# Optimizing a Trainium2 kernel written in Bass

```python
import numpy as np
import jax
import jax.numpy as jnp

def _softmax(x, axis=-1):
    return jax.nn.softmax(x, axis=axis)

def _gelu(x):
    return jax.nn.gelu(x, approximate=True)

def _silu(x):
    return jax.nn.silu(x)

def _sigmoid(x):
    return jax.nn.sigmoid(x)

def _layernorm(x, axis=-1, eps=1e-05):
    m = jnp.mean(x, axis=axis, keepdims=True)
    v = jnp.var(x, axis=axis, keepdims=True)
    return (x - m) / jnp.sqrt(v + eps)

def _scatter_add(tgt, idx, src, axis=0):
    return tgt.at[idx].add(src)

def _segment_sum(src, seg, n):
    return jax.ops.segment_sum(src, seg, n)
kernel_name = 'mk_seq_postln_d1_jaxref_r8_a663a2'

def setup_inputs(seed: int=0):
    np.random.seed(seed)
    _w = jnp.asarray

    def _L0_attn_setup():
        import jax, jax.numpy as jnp
        import numpy as np
        BATCH, SEQ, EMBED = (8, 128, 256)
        HEADS, LATENT = (16, 64)
        HEAD_DIM = EMBED // HEADS
        NOPE = HEAD_DIM // 4
        ROPE_D = HEAD_DIM - NOPE
        THETA = 10000.0

        def _rope_tables(seq_len):
            freqs = 1.0 / THETA ** (jnp.arange(0, ROPE_D, 2, dtype=jnp.float32) / ROPE_D)
            emb = jnp.arange(seq_len, dtype=jnp.float32)[:, None] * freqs[None, :]
            return (jnp.cos(emb), jnp.sin(emb))

        def _apply_rope(x, cos, sin):
            xe, xo = (x[..., ::2], x[..., 1::2])
            return jnp.concatenate([xe * cos - xo * sin, xo * cos + xe * sin], axis=-1)
        key = jax.random.key(seed)
        ks = jax.random.split(key, 5)
        x = jax.random.normal(ks[0], (BATCH, SEQ, EMBED), jnp.float32)
        Wq = jax.random.normal(ks[1], (EMBED, EMBED), jnp.float32) * 0.02
        Wkv_down = jax.random.normal(ks[2], (EMBED, LATENT), jnp.float32) * 0.02
        Wk_up = jax.random.normal(ks[3], (LATENT, EMBED), jnp.float32) * 0.02
        Wv_up = jax.random.normal(ks[4], (LATENT, EMBED), jnp.float32) * 0.02
        return {'x': x, 'Wq': Wq, 'Wkv_down': Wkv_down, 'Wk_up': Wk_up, 'Wv_up': Wv_up}
    _L0_attn_in = _L0_attn_setup()

    def _L0_ffn_setup():
        import jax, jax.numpy as jnp
        import numpy as np
        DIM = 256
        INTER = 176
        N_EXPERTS = 16
        TOP_K = 2
        N_SHARED = 2
        SHARED_INTER = N_SHARED * INTER

        def _swiglu(t, wa, wb, wo):
            h = jax.nn.silu(t @ wa.T) * (t @ wb.T)
            return h @ wo.T
        key = jax.random.key(seed)
        ks = jax.random.split(key, 9)
        s = 0.02
        return {'x': jax.random.normal(ks[0], (4, 256, DIM), dtype=jnp.float32), 'gate_w': jax.random.normal(ks[1], (N_EXPERTS, DIM), dtype=jnp.float32) * s, 'w1': jax.random.normal(ks[2], (N_EXPERTS, INTER, DIM), dtype=jnp.float32) * s, 'w2': jax.random.normal(ks[3], (N_EXPERTS, DIM, INTER), dtype=jnp.float32) * s, 'w3': jax.random.normal(ks[4], (N_EXPERTS, INTER, DIM), dtype=jnp.float32) * s, 'sw1': jax.random.normal(ks[5], (SHARED_INTER, DIM), dtype=jnp.float32) * s, 'sw2': jax.random.normal(ks[6], (DIM, SHARED_INTER), dtype=jnp.float32) * s, 'sw3': jax.random.normal(ks[7], (SHARED_INTER, DIM), dtype=jnp.float32) * s}
    _L0_ffn_in = _L0_ffn_setup()
    _d = {'L0_attn_x': _L0_attn_in['x'], 'L0_attn_Wq': _L0_attn_in['Wq'], 'L0_attn_Wkv_down': _L0_attn_in['Wkv_down'], 'L0_attn_Wk_up': _L0_attn_in['Wk_up'], 'L0_attn_Wv_up': _L0_attn_in['Wv_up'], 'L0_ffn_gate_w': _L0_ffn_in['gate_w'], 'L0_ffn_w1': _L0_ffn_in['w1'], 'L0_ffn_w2': _L0_ffn_in['w2'], 'L0_ffn_w3': _L0_ffn_in['w3'], 'L0_ffn_sw1': _L0_ffn_in['sw1'], 'L0_ffn_sw2': _L0_ffn_in['sw2'], 'L0_ffn_sw3': _L0_ffn_in['sw3']}
    _x0 = _d['L0_attn_x']
    _d['L0_attn_x'] = jax.random.normal(jax.random.fold_in(jax.random.key(seed), 1), (1, 2048, 256), dtype=_x0.dtype)
    del _x0
    return _d

def reference(L0_attn_x, L0_attn_Wq, L0_attn_Wkv_down, L0_attn_Wk_up, L0_attn_Wv_up, L0_ffn_gate_w, L0_ffn_w1, L0_ffn_w2, L0_ffn_w3, L0_ffn_sw1, L0_ffn_sw2, L0_ffn_sw3):

    def _L0_attn_ref(x, Wq, Wkv_down, Wk_up, Wv_up):
        import jax, jax.numpy as jnp
        import numpy as np
        BATCH, SEQ, EMBED = (8, 128, 256)
        HEADS, LATENT = (16, 64)
        HEAD_DIM = EMBED // HEADS
        NOPE = HEAD_DIM // 4
        ROPE_D = HEAD_DIM - NOPE
        THETA = 10000.0

        def _rope_tables(seq_len):
            freqs = 1.0 / THETA ** (jnp.arange(0, ROPE_D, 2, dtype=jnp.float32) / ROPE_D)
            emb = jnp.arange(seq_len, dtype=jnp.float32)[:, None] * freqs[None, :]
            return (jnp.cos(emb), jnp.sin(emb))

        def _apply_rope(x, cos, sin):
            xe, xo = (x[..., ::2], x[..., 1::2])
            return jnp.concatenate([xe * cos - xo * sin, xo * cos + xe * sin], axis=-1)
        B, S, E = x.shape
        q = (x @ Wq).reshape(B, S, HEADS, HEAD_DIM).transpose(0, 2, 1, 3)
        q_nope, q_rope = (q[..., :NOPE], q[..., NOPE:])
        c_kv = x @ Wkv_down
        k = (c_kv @ Wk_up).reshape(B, S, HEADS, HEAD_DIM).transpose(0, 2, 1, 3)
        v = (c_kv @ Wv_up).reshape(B, S, HEADS, HEAD_DIM).transpose(0, 2, 1, 3)
        k_nope, k_rope = (k[..., :NOPE], k[..., NOPE:])
        cos, sin = _rope_tables(S)
        q_rope = _apply_rope(q_rope, cos, sin)
        k_rope = _apply_rope(k_rope, cos, sin)
        qf = jnp.concatenate([q_nope, q_rope], axis=-1)
        kf = jnp.concatenate([k_nope, k_rope], axis=-1)
        scale = jnp.float32(1.0 / np.sqrt(HEAD_DIM))
        scores = jnp.einsum('bhqd,bhkd->bhqk', qf, kf) * scale
        causal = jnp.triu(jnp.ones((S, S), dtype=bool), k=1)
        scores = jnp.where(causal, -jnp.inf, scores)
        weights = jax.nn.softmax(scores, axis=-1)
        out = jnp.einsum('bhqk,bhkd->bhqd', weights, v)
        return out.transpose(0, 2, 1, 3).reshape(B, S, E)

    def _L0_ffn_ref(x, gate_w, w1, w2, w3, sw1, sw2, sw3):
        import jax, jax.numpy as jnp
        import numpy as np
        DIM = 256
        INTER = 176
        N_EXPERTS = 16
        TOP_K = 2
        N_SHARED = 2
        SHARED_INTER = N_SHARED * INTER

        def _swiglu(t, wa, wb, wo):
            h = jax.nn.silu(t @ wa.T) * (t @ wb.T)
            return h @ wo.T
        shape = x.shape
        t = x.reshape(-1, DIM)
        scores = jax.nn.softmax(t @ gate_w.T, axis=-1)
        weights, indices = jax.lax.top_k(scores, TOP_K)
        y = jnp.zeros_like(t)
        for e in range(N_EXPERTS):
            w_e = jnp.sum(jnp.where(indices == e, weights, 0.0), axis=-1)
            y = y + _swiglu(t, w1[e], w3[e], w2[e]) * w_e[:, None]
        z = _swiglu(t, sw1, sw3, sw2)
        return (y + z).reshape(shape)
    x = L0_attn_x
    x = _layernorm(x + _L0_attn_ref(x, L0_attn_Wq, L0_attn_Wkv_down, L0_attn_Wk_up, L0_attn_Wv_up), axis=-1)
    x = _layernorm(x + _L0_ffn_ref(x, L0_ffn_gate_w, L0_ffn_w1, L0_ffn_w2, L0_ffn_w3, L0_ffn_sw1, L0_ffn_sw2, L0_ffn_sw3), axis=-1)
    return x

_drawn_inputs = setup_inputs


def setup_inputs(seed=0):
    import zlib

    import numpy as np

    out = dict(_drawn_inputs(seed))
    spreads = {}
    factors = {'L0_attn_Wq': 8.0,
     'L0_attn_Wkv_down': 8.0,
     'L0_attn_Wk_up': 8.0,
     'L0_attn_Wv_up': 8.0,
     'L0_ffn_gate_w': 8.0,
     'L0_ffn_w1': 8.0,
     'L0_ffn_w2': 8.0,
     'L0_ffn_w3': 8.0,
     'L0_ffn_sw1': 2.893,
     'L0_ffn_sw2': 2.868,
     'L0_ffn_sw3': 2.863}
    for name, (base, spread) in spreads.items():
        noise = np.random.default_rng([zlib.crc32(name.encode()), seed]).standard_normal(out[name].shape)
        drawn = base * np.exp(spread * noise) if base else spread * noise
        out[name] = jnp.asarray(drawn.astype(out[name].dtype))
    for name, factor in factors.items():
        out[name] = (out[name] * factor).astype(out[name].dtype)
    return out
```

```python
from contextlib import ExitStack

import numpy as np

import concourse.bass as bass
from concourse import mybir

F32 = mybir.dt.float32
F32R = mybir.dt.float32r
BF16 = mybir.dt.bfloat16
I32 = mybir.dt.int32
U32 = mybir.dt.uint32
ALU = mybir.AluOpType
ACT = mybir.ActivationFunctionType
AX = mybir.AxisListType

P = 128
HEADS, DH, LATENT = 16, 16, 64
NOPE = DH // 4
ROPE_D = DH - NOPE
THETA = 10000.0
EPS = 1e-5
CH = 512
TPC = CH // P
GH = 4
UNITS_PER_CHUNK = HEADS // GH
SPLIT = 3 * DH
STACK = 2 * SPLIT
ROWS = STACK + 2
NEG = -3.0e38


def build_attention(nc, t, x1_dram):
    S, E = t["x"].shape
    NCH = S // CH
    UNITS = NCH * UNITS_PER_CHUNK
    KT = E // P
    SCALE = 1.0 / float(np.sqrt(DH))

    steps = [(u, b) for u in range(UNITS) for b in range(TPC * (u // UNITS_PER_CHUNK + 1))]
    first_step = {}
    for s, (u, b) in enumerate(steps):
        first_step.setdefault(u, s)
    first_step[UNITS] = len(steps)

    def max_banks(u):
        c = u // UNITS_PER_CHUNK
        return [(u, h, i, kb) for h in range(GH) for i in range(TPC) for kb in range(c + 1)]

    def projection_jobs(c):
        return [("latent", c, 0), ("rope", c, 0), ("rope", c, 1), ("rope", c, 2), ("rope", c, 3),
                ("rope", c, 4), ("rope", c, 5), ("rope", c, 6), ("rope", c, 7), ("value", c, 0), ("value", c, 1)]

    prologue = projection_jobs(0) + [("maxima", 0), ("maxima", 1)]
    aux_at = {s: [] for s in range(len(steps) + 1)}
    max_at = {s: [] for s in range(len(steps))}
    for k, job in enumerate(projection_jobs(1)):
        aux_at[k // 2].append(job)
    for u in range(UNITS):
        s0, n = first_step[u], first_step[u + 1] - first_step[u]
        if u + 2 < UNITS:
            banks = max_banks(u + 2)
            for k in range(n):
                max_at[s0 + k] = banks[k * len(banks) // n:(k + 1) * len(banks) // n]
        if 2 <= u + 1 < UNITS:
            aux_at[s0].append(("maxima", u + 1))
        if u >= 1:
            aux_at[s0 + 2].append(("out", u - 1))
    aux_at[len(steps)].append(("out", UNITS - 1))
    for c in range(2, NCH):
        s0 = first_step[(c - 1) * UNITS_PER_CHUNK]
        for k, job in enumerate(projection_jobs(c)):
            aux_at[s0 + 1 + k].append(job)
    aux_order = prologue + [j for s in range(len(steps) + 1) for j in aux_at[s]]
    aux_no = {j: n + 1 for n, j in enumerate(aux_order)}
    max_order = max_banks(0) + max_banks(1) + [m for s in range(len(steps)) for m in max_at[s]]
    max_no = {m: n + 1 for n, m in enumerate(max_order)}
    diag_before = [0]
    for u, b in steps:
        diag_before.append(diag_before[-1] + 2 * (b >= TPC * (u // UNITS_PER_CHUNK)))

    kq_dram = nc.dram_tensor("kq_split", (NCH, 4, 2, P, CH), F32, kind="Internal").ap()

    with ExitStack() as ctx:
        def sb(name, shape, dt=F32):
            return ctx.enter_context(nc.sbuf_tensor(name, shape, dt))

        def ps(name, shape):
            return ctx.enter_context(nc.psum_tensor(name, shape, F32))

        def sem(name):
            return ctx.enter_context(nc.semaphore(name))

        k_stack = sb("k_stack", [ROWS, HEADS // 2, S], F32R)
        q_stack = sb("q_stack", [ROWS, 4, GH, CH], F32R)
        v_ones = sb("v_ones", [P, S // P, HEADS, DH + 1])
        probs = sb("probs", [P, 4, 2, CH])
        w_raw = sb("w_raw", [P, 2048])
        w_split = sb("w_split", [P, 2, 2048], F32R)
        x_raw = sb("x_raw", [P, KT, CH])
        x_split = sb("x_split", [P, 2, KT, CH], F32R)
        rope = sb("rope_sb", [P, 2, CH])
        latent = sb("latent", [P, CH], F32R)
        latent_hi = sb("latent_hi", [P, CH], F32R)
        by_cos = sb("by_cos", [P, 256])
        by_sin = sb("by_sin", [P, 256])
        roped = sb("roped", [P, 2, 256])
        kq_stage = sb("kq_stage", [P, 2, 2, CH], F32R)
        ident = sb("ident", [P, P])
        ident_b = sb("ident_b", [P, P], BF16)
        mask_b = sb("mask_b", [P, P], BF16)
        mx = sb("mx", [P, 2, GH * TPC, 4])
        mx_row = sb("mx_row", [P, 2, GH * TPC])
        m_rows = sb("m_rows", [GH * TPC, 2, 2, P], F32R)
        out_t = sb("out_t", [P, CH])
        recip = sb("recip", [P, TPC, GH])
        attn = sb("attn", [P, TPC, E])
        x_tok = sb("x_tok", [P, TPC, E])
        summed = sb("summed", [P, TPC, E])
        stats = sb("stats", [P, TPC, 6])
        mean_var = sb("mean_var", [P, TPC, 2])
        power = sb("power", [P, TPC])
        var_eps = sb("var_eps", [P, TPC])
        rstd = sb("rstd", [P, TPC])

        scores = ps("scores", [P, 2, 2, CH])
        max_ps = ps("max_ps", [P, 2, CH])
        pv_ps = ps("pv_ps", [P, CH])
        aux_ps = ps("aux_ps", [P, CH])

        OFF_Q, OFF_D, OFF_K, OFF_V = 0, 1024, 1280, 1792
        wq = w_split[:, :, OFF_Q:OFF_D].rearrange("p s (k n) -> p s k n", k=KT)
        wd = w_split[:, :, OFF_D:OFF_K].rearrange("p s (k n) -> p s k n", k=KT)
        wk = w_split[:, :, OFF_K:OFF_V]
        wv = w_split[:, :, OFF_V:2048]

        w_loaded = sem("w_loaded")
        x_loaded = sem("x_loaded")
        rope_loaded = sem("rope_loaded")
        tok_loaded = sem("tok_loaded")
        kq_stored = sem("kq_stored")
        k_stacked = sem("k_stacked")
        q_stacked = sem("q_stacked")
        m_stacked = sem("m_stacked")
        consts_ready = sem("consts_ready")
        dve_consts = sem("dve_consts")
        zeros_low = sem("zeros_low")
        zeros_high = sem("zeros_high")
        ones_first = sem("ones_first")
        ones_ready = sem("ones_ready")
        w_ready = sem("w_ready")
        x_ready = sem("x_ready")
        pe_scores = sem("pe_scores")
        pe_max = sem("pe_max")
        pe_pv = sem("pe_pv")
        pe_aux = sem("pe_aux")
        exp_done = sem("exp_done")
        mask_done = sem("mask_done")
        max_done = sem("max_done")
        aux_done = sem("aux_done")
        roped_ready = sem("roped_ready")
        kq_ready = sem("kq_ready")
        mx_ready = sem("mx_ready")
        pv_done = sem("pv_done")
        dve_chain = sem("dve_chain")
        pool_chain = sem("pool_chain")
        var_ready = sem("var_ready")
        rstd_ready = sem("rstd_ready")
        x1_ready = sem("x1_ready")
        x1_stored = sem("x1_stored")

        block = ctx.enter_context(nc.Block())

        def aux_bank(job):
            n = aux_no[job]
            return scores[:, 1, 1] if n <= len(prologue) and n % 2 == 0 else aux_ps[:]

        def rope_after(c):
            return 8 * (c + 1)

        @block.sync
        def _(sp):
            sp.dma_start(x_raw[:], t["xT"][:, 0:CH].rearrange("(k p) n -> p k n", p=P)).then_inc(x_loaded, 16)
            sp.dma_start(w_raw[:, OFF_D:OFF_K].rearrange("p (k n) -> p k n", k=KT),
                         t["w_down"].rearrange("(k p) n -> p k n", p=P)).then_inc(w_loaded, 16)
            sp.dma_start(w_raw[:, OFF_Q:OFF_D].rearrange("p (k n) -> p k n", k=KT),
                         t["w_q"].rearrange("(k p) n -> p k n", p=P)).then_inc(w_loaded, 16)
            sp.dma_start(w_raw[:, OFF_K:OFF_V], t["w_k"]).then_inc(w_loaded, 16)
            sp.dma_start(w_raw[:, OFF_V:2048], t["w_v"]).then_inc(w_loaded, 16)
            sp.dma_start(rope[:], t["rope"][:, :, 0:CH]).then_inc(rope_loaded, 16)
            def load_q(u):
                c, g = divmod(u, UNITS_PER_CHUNK)
                m, j0 = g // 2, GH * (g % 2)
                if u == 0:
                    sp.wait_ge(zeros_low, 1)
                if u == 2:
                    sp.wait_ge(zeros_high, 1)
                if u:
                    sp.wait_ge(q_stacked, 16 * 6 * u)
                if u >= 4:
                    sp.wait_ge(pe_scores, 2 * first_step[u - 3])
                for par in range(2):
                    for copy, part in enumerate((0, 1, 0)):
                        r = par * SPLIT + copy * DH
                        src = kq_dram[c, 2 * m + 1, part].rearrange("(j two d) n -> two d j n", two=2, d=DH)
                        sp.dma_start(q_stack[r:r + DH, u % 4, par::2, :].bitcast(F32),
                                     src[par, :, j0 // 2:j0 // 2 + 2, :]).then_inc(q_stacked, 16)

            piece = 0
            for c in range(NCH):
                if c + 1 < NCH:
                    sp.wait_ge(x_ready, c + 1)
                    sp.dma_start(x_raw[:], t["xT"][:, (c + 1) * CH:(c + 2) * CH].rearrange("(k p) n -> p k n", p=P))\
                      .then_inc(x_loaded, 16)
                for n in range(4):
                    m, is_q = n // 2, n % 2
                    sp.wait_ge(kq_ready, 2 * (piece + 1))
                    sp.dma_start(kq_dram[c, n].rearrange("s p n -> p s n"), kq_stage[:, piece % 2].bitcast(F32)).then_inc(kq_stored, 16)
                    piece += 1
                    sp.wait_ge(kq_stored, 16 * piece)
                    if not is_q:
                        if piece > 1:
                            sp.wait_ge(k_stacked, 16 * 6 * (piece // 2))
                        for par in range(2):
                            for copy, part in enumerate((0, 0, 1)):
                                r = par * SPLIT + copy * DH
                                src = kq_dram[c, n, part].rearrange("(j two d) n -> two d j n", two=2, d=DH)
                                sp.dma_start(k_stack[r:r + DH, 4 * m:4 * m + 4, c * CH:(c + 1) * CH].bitcast(F32),
                                             src[par]).then_inc(k_stacked, 16)
                    elif c == 0:
                        load_q(2 * m)
                        load_q(2 * m + 1)
                if c + 1 < NCH:
                    sp.wait_ge(roped_ready, rope_after(c))
                    sp.dma_start(rope[:], t["rope"][:, :, (c + 1) * CH:(c + 2) * CH]).then_inc(rope_loaded, 16)
                if c > 0:
                    for g in range(UNITS_PER_CHUNK):
                        load_q(c * UNITS_PER_CHUNK + g)
            sp.wait_ge(x1_stored, 16 * NCH)

        @block.gpsimd
        def _(pool):
            chain = [0]

            def link(ins):
                chain[0] += 1
                ins.then_inc(pool_chain, 1)
                pool.wait_ge(pool_chain, chain[0])

            def split(hi, lo, src, done):
                link(nc.gpsimd.tensor_scalar(hi, src, 1.0, 0.0, ALU.mult, ALU.add))
                nc.gpsimd.tensor_tensor(lo, src, hi.bitcast(F32), ALU.subtract).then_inc(done, 1)

            def split_x(c):
                pool.wait_ge(x_loaded, 16 * (c + 1))
                if c:
                    pool.wait_ge(pe_aux, aux_no[("rope", c - 1, 7)])
                split(x_split[:, 0], x_split[:, 1], x_raw[:], x_ready)

            def load_tokens(c):
                pool.dma_start(x_tok[:], t["x"][c * CH:(c + 1) * CH, :].rearrange("(i p) n -> p i n", p=P))\
                    .then_inc(tok_loaded, 16)

            load_tokens(0)
            split_x(0)
            pool.wait_ge(w_loaded, 64)
            split(w_split[:, 0], w_split[:, 1], w_raw[:], w_ready)
            nc.gpsimd.memset(q_stack[0:STACK, 2:4].bitcast(F32), 0.0).then_inc(zeros_high, 1)
            link(nc.gpsimd.memset(ident[:], 0.0))
            link(nc.gpsimd.affine_select(out=ident[:], in_=ident[:], compare_op=ALU.not_equal, fill=1.0, base=0,
                                         pattern=[[-1, P]], channel_multiplier=1))
            nc.gpsimd.tensor_copy(ident_b[:], ident[:]).then_inc(consts_ready, 1)
            link(nc.gpsimd.memset(mask_b[:], 0.0))
            nc.gpsimd.affine_select(out=mask_b[:], in_=mask_b[:], compare_op=ALU.is_ge, fill=NEG, base=0,
                                    pattern=[[-1, P]], channel_multiplier=1).then_inc(consts_ready, 1)
            link(nc.gpsimd.memset(power[:], -0.5))

            def split_rope(c, n):
                k = 8 * c + n
                pool.wait_ge(roped_ready, k + 1)
                piece = k // 2
                if piece >= 2 and n % 2 == 0:
                    pool.wait_ge(kq_stored, 16 * (piece - 1))
                cols = slice(256 * (n % 2), 256 * (n % 2) + 256)
                split(kq_stage[:, piece % 2, 0, cols], kq_stage[:, piece % 2, 1, cols], roped[:, k % 2], kq_ready)

            def inverse_deviation(c):
                pool.wait_ge(var_ready, c + 1)
                nc.gpsimd.tensor_tensor(rstd[:], var_eps[:], power[:], ALU.pow).then_inc(rstd_ready, 1)
                pool.wait_ge(x1_ready, c + 1)
                pool.dma_start(x1_dram[c * CH:(c + 1) * CH, :].rearrange("(i p) n -> p i n", p=P), summed[:])\
                    .then_inc(x1_stored, 16)
                if c + 1 < NCH:
                    load_tokens(c + 1)

            def own_part(jobs):
                for job in jobs:
                    if job[0] == "out" and job[1] % UNITS_PER_CHUNK == UNITS_PER_CHUNK - 1:
                        inverse_deviation(job[1] // UNITS_PER_CHUNK)
                    if job[0] == "rope":
                        split_rope(job[1], job[2])
                    if job[0] == "value" and job[2] == 1 and job[1] + 1 < NCH:
                        c = job[1] + 1
                        split_x(c)
                        pool.wait_ge(x_ready, c + 1)
                        nc.gpsimd.memset(k_stack[STACK:ROWS, :, c * CH:(c + 1) * CH].bitcast(F32), 1.0)\
                            .then_inc(ones_ready, 1)
                        pool.wait_ge(ones_ready, c)

            def mask(s):
                u, b = steps[s]
                c = u // UNITS_PER_CHUNK
                if b < TPC * c:
                    return
                off = P * (b - TPC * c)
                for half in range(2):
                    pool.wait_ge(exp_done, 2 * s + half + 1)
                    v = probs[:, (2 * s + half) % 4, :, off:off + P]
                    nc.gpsimd.affine_select(out=v, in_=v, compare_op=ALU.is_ge, fill=0.0, base=0,
                                            pattern=[[0, 2], [1, P]], channel_multiplier=-1).then_inc(mask_done, 1)

            own_part(prologue)
            for s in range(len(steps)):
                mask(s)
                own_part(aux_at[s])
            own_part(aux_at[len(steps)])

        @block.scalar
        def _(act):
            def store_maxima(u):
                act.wait_ge(aux_done, aux_no[("maxima", u)])
                if u:
                    act.wait_ge(m_stacked, 32 * u)
                for part in range(2):
                    act.dma_start(q_stack[STACK + part:STACK + part + 1, u % 4].rearrange("o h n -> o (h n)").bitcast(F32),
                                  m_rows[:, u % 2, part, :].bitcast(F32)).then_inc(m_stacked, 16)

            store_maxima(0)
            store_maxima(1)
            for s, (u, b) in enumerate(steps):
                c = u // UNITS_PER_CHUNK
                off = max(0, P * (b - TPC * c))
                for half in range(2):
                    n = 2 * s + half
                    act.wait_ge(pe_scores, n + 1)
                    if s >= 2:
                        act.wait_ge(pe_pv, s - 1)
                    nc.scalar.activation(probs[:, n % 4, :, off:CH], scores[:, n % 2, :, off:CH], ACT.Exp)\
                      .then_inc(exp_done, 1)
                for job in aux_at[s]:
                    if job[0] == "maxima":
                        store_maxima(job[1])

        @block.tensor
        def _(pe):
            def aux_free(job):
                n = aux_no[job]
                if n > len(prologue):
                    pe.wait_ge(aux_done, n - 1)
                elif n > 2:
                    pe.wait_ge(aux_done, n - 2)
                return aux_bank(job)

            def projection(job):
                kind, c, n = job
                if kind == "latent":
                    pe.wait_ge(x_ready, c + 1)
                    if c == 0:
                        pe.wait_ge(w_ready, 1)
                    aux = aux_free(job)
                    k = 0
                    for kt in range(KT):
                        for a, b in ((0, 0), (0, 1), (1, 0)):
                            last = nc.tensor.matmul(aux, wd[:, a, kt, :], x_split[:, b, kt, :],
                                                    start=(k == 0), stop=(k == 3 * KT - 1))
                            k += 1
                    last.then_inc(pe_aux, 1)
                elif kind == "rope":
                    piece, half = n // 2, n % 2
                    m, is_q = piece // 2, piece % 2
                    cols = slice(256 * half, 256 * half + 256)
                    if n == 0:
                        pe.wait_ge(aux_done, aux_no[("latent", c, 0)])
                    aux = aux_free(job)
                    for partner in range(2):
                        dst = aux[:, 256 * partner:256 * partner + 256]
                        w0 = 256 * partner + P * m
                        if is_q:
                            k = 0
                            for kt in range(KT):
                                for a, b in ((0, 0), (0, 1), (1, 0)):
                                    last = nc.tensor.matmul(dst, wq[:, a, kt, w0:w0 + P], x_split[:, b, kt, cols],
                                                            start=(k == 0), stop=(k == 3 * KT - 1))
                                    k += 1
                        else:
                            for a in range(2):
                                last = nc.tensor.matmul(dst, wk[:, a, w0:w0 + P], latent[:, cols],
                                                        start=(a == 0), stop=(a == 1))
                    last.then_inc(pe_aux, 1)
                else:
                    aux = aux_free(job)
                    for i in range(2):
                        tok = slice((2 * n + i) * P, (2 * n + i + 1) * P)
                        for a in range(2):
                            last = nc.tensor.matmul(aux[:, 256 * i:256 * i + 256], latent[:, tok], wv[:, a, :],
                                                    start=(a == 0), stop=(a == 1))
                    last.then_inc(pe_aux, 1)

            def run_aux(job):
                if job[0] == "maxima":
                    pe.wait_ge(mx_ready, job[1] + 1)
                    aux = aux_free(job)
                    nc.tensor.transpose(aux[0:GH * TPC, 0:P], mx_row[:, job[1] % 2, :], ident[:]).then_inc(pe_aux, 1)
                elif job[0] == "out":
                    pe.wait_ge(pv_done, job[1] + 1)
                    aux = aux_free(job)
                    for i in range(TPC):
                        last = nc.tensor.transpose(aux[:, P * i:P * i + P], out_t[:, P * i:P * i + P], ident[:])
                    last.then_inc(pe_aux, 1)
                else:
                    projection(job)

            def max_bank(bank):
                u, h, i, kb = bank
                c = u // UNITS_PER_CHUNK
                n = max_no[bank]
                pair = (u % UNITS_PER_CHUNK) * 2 + h // 2
                if n > 2:
                    pe.wait_ge(max_done, n - 2)
                last = kb == c
                cols = (i + 1) * P if last else CH
                ins = nc.tensor.matmul(max_ps[:, n % 2, 0:cols], q_stack[0:STACK, u % 4, h, i * P:(i + 1) * P],
                                       k_stack[0:STACK, pair, kb * CH:kb * CH + cols], start=True, stop=not last)
                if last:
                    ins = nc.tensor.matmul(max_ps[:, n % 2, i * P:(i + 1) * P], ident_b[:], mask_b[:],
                                           start=False, stop=True)
                ins.then_inc(pe_max, 1)

            def max_unit(u):
                c, g = divmod(u, UNITS_PER_CHUNK)
                pe.wait_ge(k_stacked, 16 * 6 * (2 * c + g // 2 + 1))
                pe.wait_ge(q_stacked, 16 * 6 * (u + 1))

            def score_half(s, half):
                u, b = steps[s]
                c, g = divmod(u, UNITS_PER_CHUNK)
                off = max(0, P * (b - TPC * c))
                n = 2 * s + half
                if n == 0:
                    pe.wait_ge(aux_done, len(prologue))
                if n >= 2:
                    pe.wait_ge(exp_done, n - 1)
                if b == 0 and half == 0:
                    pe.wait_ge(m_stacked, 32 * (u + 1))
                    pe.wait_ge(ones_first, 1)
                    if c:
                        pe.wait_ge(ones_ready, c)
                for k in range(2):
                    h = 2 * half + k
                    last = nc.tensor.matmul(scores[:, n % 2, k, off:CH], k_stack[:, 2 * g + half, b * P:(b + 1) * P],
                                            q_stack[:, u % 4, h, off:CH], start=True, stop=True)
                last.then_inc(pe_scores, 1)

            def values(s, part):
                u, b = steps[s]
                c, g = divmod(u, UNITS_PER_CHUNK)
                off = max(0, P * (b - TPC * c))
                lo, hi = max(off, 256 * part), 256 * part + 256
                if lo >= hi:
                    return
                pe.wait_ge(exp_done, 2 * s + 2)
                if b >= TPC * c:
                    pe.wait_ge(mask_done, diag_before[s + 1])
                if b == 0:
                    if u:
                        pe.wait_ge(pv_done, u)
                    else:
                        pe.wait_ge(dve_consts, 2)
                    if g == 0:
                        pe.wait_ge(aux_done, aux_no[("value", c, 1)])
                for h in range(GH):
                    last = nc.tensor.matmul(pv_ps[32 * h:32 * h + DH + 1, lo:hi], v_ones[:, b, GH * g + h, :],
                                            probs[:, (2 * s + h // 2) % 4, h % 2, lo:hi],
                                            start=(b == 0 and part == 0), stop=(b == TPC * (c + 1) - 1),
                                            skip_group_check=True)
                if part:
                    last.then_inc(pe_pv, 1)

            for job in prologue:
                if job[0] == "maxima":
                    pe.wait_ge(consts_ready, 2)
                    max_unit(job[1])
                    for bank in max_banks(job[1]):
                        max_bank(bank)
                run_aux(job)
            for s, (u, b) in enumerate(steps):
                if b == 0 and u + 2 < UNITS:
                    max_unit(u + 2)
                banks, jobs = max_at[s], aux_at[s]
                n, quarter = len(banks), [len(banks) * k // 4 for k in range(5)]
                for k in range(4):
                    for bank in banks[quarter[k]:quarter[k + 1]]:
                        max_bank(bank)
                    if k in (0, 2):
                        score_half(s, k // 2)
                    else:
                        if s:
                            values(s - 1, k // 2)
                        for job in (jobs[:(len(jobs) + 1) // 2] if k == 1 else jobs[(len(jobs) + 1) // 2:]):
                            run_aux(job)
            for part in range(2):
                values(len(steps) - 1, part)
            for job in aux_at[len(steps)]:
                run_aux(job)

        @block.vector
        def _(dve):
            chain = [0]

            def link(ins):
                chain[0] += 1
                ins.then_inc(dve_chain, 1)
                dve.wait_ge(dve_chain, chain[0])

            nc.vector.memset(pv_ps[:], 0.0).then_inc(dve_consts, 1)
            nc.vector.memset(v_ones[:, :, :, DH:DH + 1], 1.0).then_inc(dve_consts, 1)
            nc.vector.memset(q_stack[0:STACK, 0:2].bitcast(F32), 0.0).then_inc(zeros_low, 1)
            nc.vector.memset(k_stack[STACK:ROWS, :, 0:CH].bitcast(F32), 1.0).then_inc(ones_first, 1)

            def reduce_bank(bank):
                u, h, i, kb = bank
                c = u // UNITS_PER_CHUNK
                n = max_no[bank]
                cols = (i + 1) * P if kb == c else CH
                if u >= 2 and (h, i, kb) == (0, 0, 0):
                    dve.wait_ge(mx_ready, u - 1)
                dve.wait_ge(pe_max, n)
                nc.vector.tensor_reduce(mx[:, u % 2, h * TPC + i, kb:kb + 1], max_ps[:, n % 2, 0:cols], AX.X, ALU.max)\
                  .then_inc(max_done, 1)

            def fold_maxima(u):
                c = u // UNITS_PER_CHUNK
                dve.wait_ge(max_done, max_no[max_banks(u)[-1]])
                if u >= 2:
                    dve.wait_ge(pe_aux, aux_no[("maxima", u - 2)])
                nc.vector.tensor_reduce(mx_row[:, u % 2, :], mx[:, u % 2, :, 0:c + 1], AX.X, ALU.max)\
                  .then_inc(mx_ready, 1)

            def run_aux(job):
                dve.wait_ge(pe_aux, aux_no[job])
                kind = job[0]
                aux = aux_bank(job)
                if kind == "latent":
                    if job[1]:
                        dve.wait_ge(pe_aux, aux_no[("value", job[1] - 1, 1)])
                        dve.wait_ge(aux_done, aux_no[("latent", job[1] - 1, 0)])
                    link(nc.vector.tensor_copy(latent_hi[LATENT:P], aux[LATENT:P]))
                    link(nc.vector.tensor_copy(latent[0:LATENT], aux[0:LATENT]))
                    nc.vector.tensor_tensor(latent[LATENT:P], aux[LATENT:P], latent_hi[LATENT:P].bitcast(F32),
                                            ALU.subtract).then_inc(aux_done, 1)
                elif kind == "rope":
                    c, n = job[1:]
                    k = 8 * c + n
                    scale = SCALE if (n // 2) % 2 else 1.0
                    cols = slice(256 * (n % 2), 256 * (n % 2) + 256)
                    if n == 0:
                        dve.wait_ge(rope_loaded, 16 * (c + 1))
                    if k:
                        dve.wait_ge(roped_ready, k)
                    nc.vector.scalar_tensor_tensor(out=by_cos[:], in0=aux[:, 0:256], scalar=scale,
                                                   in1=rope[:, 0, cols], op0=ALU.mult, op1=ALU.mult)
                    nc.vector.scalar_tensor_tensor(out=by_sin[:], in0=aux[:, 256:512], scalar=scale,
                                                   in1=rope[:, 1, cols], op0=ALU.mult, op1=ALU.mult)\
                      .then_inc(aux_done, 1)
                    dve.wait_ge(aux_done, aux_no[job])
                    if k >= 2:
                        dve.wait_ge(kq_ready, k - 1)
                    nc.vector.tensor_tensor(roped[:, k % 2], by_cos[:], by_sin[:], ALU.add).then_inc(roped_ready, 1)
                elif kind == "value":
                    c, n = job[1:]
                    nc.vector.tensor_copy(v_ones[:, TPC * c + 2 * n:TPC * c + 2 * n + 2, :, 0:DH],
                                          aux.rearrange("p (t h d) -> p t h d", t=2, h=HEADS)).then_inc(aux_done, 1)
                elif kind == "maxima":
                    u = job[1]
                    src = aux[0:GH * TPC, 0:P]
                    if u >= 2:
                        dve.wait_ge(m_stacked, 32 * (u - 1))
                    link(nc.vector.tensor_scalar(m_rows[:, u % 2, 0, :], src, -1.0, None, ALU.mult))
                    nc.vector.scalar_tensor_tensor(out=m_rows[:, u % 2, 1, :], in0=src, scalar=-1.0,
                                                   in1=m_rows[:, u % 2, 0, :].bitcast(F32), op0=ALU.mult,
                                                   op1=ALU.subtract).then_inc(aux_done, 1)
                else:
                    normalise(job[1])

            def copy_output(u):
                dve.wait_ge(pe_pv, first_step[u + 1])
                if u:
                    dve.wait_ge(pe_aux, aux_no[("out", u - 1)])
                nc.vector.tensor_copy(out_t[:], pv_ps[:]).then_inc(pv_done, 1)

            def normalise(u):
                c, g = divmod(u, UNITS_PER_CHUNK)
                v = aux_ps[:].rearrange("p (i h d) -> p i h d", i=TPC, h=GH)
                if u:
                    dve.wait_ge(aux_done, aux_no[("out", u - 1)])
                link(nc.vector.reciprocal(recip[:], v[:, :, :, DH]))
                if g == 0 and c:
                    dve.wait_ge(x1_ready, c)
                a = attn[:, :, g * GH * DH:(g + 1) * GH * DH].rearrange("p i (h d) -> p i h d", h=GH)
                nc.vector.tensor_tensor(a, v[:, :, :, 0:DH],
                                        recip[:].unsqueeze(3).to_broadcast([P, TPC, GH, DH]), ALU.mult)\
                  .then_inc(aux_done, 1)
                if g == UNITS_PER_CHUNK - 1:
                    layer_norm(c, aux_no[("out", u)])

            def layer_norm(c, turn):
                dve.wait_ge(aux_done, turn)
                dve.wait_ge(tok_loaded, 16 * (c + 1))
                if c:
                    dve.wait_ge(x1_stored, 16 * c)
                link(nc.vector.tensor_tensor(summed[:], attn[:], x_tok[:], ALU.add))
                for i in range(TPC):
                    link(nc.vector.bn_stats(stats[:, i, :], summed[:, i, :]))
                for i in range(TPC):
                    link(nc.vector.bn_aggr(mean_var[:, i, :], stats[:, i, :]))
                nc.vector.tensor_scalar(var_eps[:], mean_var[:, :, 1], EPS, None, ALU.add).then_inc(var_ready, 1)
                dve.wait_ge(rstd_ready, c + 1)
                for i in range(TPC):
                    last = nc.vector.tensor_scalar(summed[:, i, :], summed[:, i, :], mean_var[:, i, 0:1],
                                                   rstd[:, i:i + 1], ALU.subtract, ALU.mult)
                last.then_inc(x1_ready, 1)

            for job in prologue:
                if job[0] == "maxima":
                    for bank in max_banks(job[1]):
                        reduce_bank(bank)
                    fold_maxima(job[1])
                run_aux(job)
            for s, (u, b) in enumerate(steps):
                banks, jobs = max_at[s], aux_at[s]
                quarter = [len(banks) * k // 4 for k in range(5)]
                for k in range(4):
                    for bank in banks[quarter[k]:quarter[k + 1]]:
                        reduce_bank(bank)
                    if k % 2:
                        for job in (jobs[:(len(jobs) + 1) // 2] if k == 1 else jobs[(len(jobs) + 1) // 2:]):
                            run_aux(job)
                if s + 1 == first_step[u + 1] and u + 2 < UNITS:
                    fold_maxima(u + 2)
                if b == 0 and u:
                    copy_output(u - 1)
            copy_output(UNITS - 1)
            for job in aux_at[len(steps)]:
                run_aux(job)


INTER = 176
EXPERTS = 16
TOP_K = 2
HALF = INTER // 2
RANKS_AT = 8
RING = 4


def build_experts(nc, t, x1_dram, out):
    S, E = out.shape
    TT = S // P
    KT = E // P
    SLOTS = (S * TOP_K + EXPERTS * (P - 1)) // P
    SHARED = 2 * TT
    ITEMS = SHARED + SLOTS

    slot_x = nc.dram_tensor("slot_x", (SLOTS * P, E), F32, kind="Internal").ap()
    slot_y = nc.dram_tensor("slot_y", (SLOTS * P, E), F32, kind="Internal").ap()

    with ExitStack() as ctx:
        def sb(name, shape, dt=F32):
            return ctx.enter_context(nc.sbuf_tensor(name, shape, dt))

        def ps(name, shape):
            return ctx.enter_context(nc.psum_tensor(name, shape, F32))

        def sem(name):
            return ctx.enter_context(nc.semaphore(name))

        w_up = sb("w_up_sb", [P, EXPERTS + 2, KT, 2 * INTER])
        w_dn = sb("w_dn_sb", [HALF, EXPERTS + 2, 2, E])
        x1 = sb("x1_sb", [P, TT, E])
        x1_t = sb("x1_t", [P, KT, S])
        base = sb("base", [P, TT, E])
        gate = sb("gate_sb", [P, KT, EXPERTS])
        consts = sb("consts_sb", [P, 16 + 16 + 256 + 48])
        ident = sb("ident2", [P, P])
        before_b = sb("before_b", [P, P], BF16)
        ones_b = sb("ones_b", [P, P], BF16)
        zeros = sb("zeros", [P, E])
        power = sb("power2", [P, TPC])
        shifted = sb("shifted", [P, TT, EXPERTS])
        probs = sb("probs2", [P, TT, EXPERTS])
        row = sb("row", [P, 4, TT])
        best = sb("best", [P, TT, 8])
        best_at = sb("best_at", [P, TT, 8], U32)
        best_f = sb("best_f", [P, 2, TT])
        chosen = sb("chosen", [P, 2, TT, EXPERTS])
        member = sb("member", [P, TT + 1, EXPERTS], BF16)
        count = sb("count", [P, EXPERTS])
        grid = sb("grid", [P, EXPERTS, TT])
        tiles = sb("tiles", [P, 3, EXPERTS])
        grid2 = sb("grid2", [P, 48, EXPERTS])
        expert_f = sb("expert_f", [P, 48])
        expert = sb("expert", [P, 48], I32)
        place = sb("place", [P, TT, EXPERTS])
        place_of = sb("place_of", [P, TT, EXPERTS])
        slot_f = sb("slot_f", [P, 2, TT])
        slot = sb("slot", [P, 2, TT], I32)
        xg = sb("xg", [P, RING, E])
        xg_t = sb("xg_t", [P, 2, KT, P])
        silu = sb("silu", [P, 2, INTER])
        hidden = sb("hidden", [P, 2, INTER])
        hidden_t = sb("hidden_t", [HALF, 2, 2, P])
        ys = sb("ys", [P, RING, E])
        yg = sb("yg", [P, 2, TPC, 2, E])
        stats = sb("stats2", [P, TPC, 6])
        mean_var = sb("mean_var2", [P, TPC, 2])
        var_eps = sb("var_eps2", [P, TPC])
        rstd = sb("rstd2", [P, TPC])

        xt_ps = ps("xt_ps", [P, 2, 512])
        gu_ps = ps("gu_ps", [P, 2, 512])
        ht_ps = ps("ht_ps", [P, 2, 512])
        y_ps = ps("y_ps", [P, 2, 512])

        small_loaded = sem("small_loaded")
        x1_loaded = sem("x1_loaded")
        shared_loaded = sem("shared_loaded")
        experts_loaded = sem("experts_loaded")
        zeros_ready = sem("zeros_ready")
        slots_cleared = sem("slots_cleared")
        consts2_ready = sem("consts2_ready")
        pe_x1t = sem("pe_x1t")
        x1t_copied = sem("x1t_copied")
        x1t_even = sem("x1t_even")
        pe_logits = sem("pe_logits")
        shift_ready = sem("shift_ready")
        exps_ready = sem("exps_ready")
        members_ready = sem("members_ready")
        pe_ranks = sem("pe_ranks")
        slots_ready = sem("slots_ready")
        experts_ready = sem("experts_ready")
        scattered = sem("scattered")
        chain_sem = sem("dve_chain2")
        xg_loaded = [sem(f"xg_loaded{r}") for r in range(RING)]
        ys_stored = [sem(f"ys_stored{r}") for r in range(RING)]
        pe_xt = sem("pe_xt")
        xt_copied = sem("xt_copied")
        pe_gu = sem("pe_gu")
        silu_done = sem("silu_done")
        hidden_done = sem("hidden_done")
        pe_ht = sem("pe_ht")
        ht_copied = sem("ht_copied")
        pe_y = sem("pe_y")
        y_taken = sem("y_taken")
        gathered = [sem(f"gathered{r}") for r in range(2)]
        sums_ready = sem("sums_ready")
        var2_ready = sem("var2_ready")
        rstd2_ready = sem("rstd2_ready")
        rows_ready = sem("rows_ready")
        rows_stored = sem("rows_stored")

        iota_e = consts[:, 0:16]
        step_128 = consts[:, 16:32]
        earlier = consts[:, 32:288].rearrange("p (e f) -> p e f", e=EXPERTS)
        iota_slot = consts[:, 288:336]

        LEAD = RING + 2
        TURNS = (SLOTS - 1 - LEAD) // RING
        LOOP_END = LEAD + RING * TURNS

        block = ctx.enter_context(nc.Block())

        def over_slots(eng, body, end):
            for j in range(LEAD):
                body(j, j % RING, j)
            with eng.Fori(0, TURNS) as turn:
                for k in range(RING):
                    body(turn * RING + (LEAD + k), (LEAD + k) % RING, LEAD + k)
            for j in range(LOOP_END, end):
                body(j, j % RING, j)

        @block.sync
        def _(sp):
            sp.dma_start(x1[:], x1_dram.rearrange("(i p) n -> p i n", p=P)).then_inc(x1_loaded, 16)
            sp.dma_start(gate[:], t["gate"]).then_inc(small_loaded, 16)
            sp.dma_start(consts[:], t["consts"]).then_inc(small_loaded, 16)
            sp.dma_start(w_up[:, EXPERTS:], t["w_up"][:, EXPERTS:]).then_inc(shared_loaded, 16)
            sp.dma_start(w_dn[:, EXPERTS:], t["w_dn"][:, EXPERTS:]).then_inc(shared_loaded, 16)
            sp.wait_ge(zeros_ready, 1)
            for j in range(0, SLOTS, 8):
                n = min(8, SLOTS - j)
                sp.dma_start(slot_x[j * P:(j + n) * P].rearrange("(i p) n -> p i n", p=P),
                             zeros[:].unsqueeze(1).to_broadcast([P, n, E])).then_inc(slots_cleared, 16)
            for e in range(0, EXPERTS, 4):
                sp.dma_start(w_up[:, e:e + 4], t["w_up"][:, e:e + 4]).then_inc(experts_loaded, 16)
                sp.dma_start(w_dn[:, e:e + 4], t["w_dn"][:, e:e + 4]).then_inc(experts_loaded, 16)
            sp.wait_ge(scattered, 16 * TOP_K * TT)

            def load(j, r, j0):
                if j0 >= RING:
                    sp.wait_ge(pe_xt, j + (1 - RING))
                sp.dma_start(xg[:, r, :], slot_x[bass.ds(j * P, P), :]).then_inc(xg_loaded[r], 16)

            over_slots(sp, load, SLOTS)
            for b in range(TT // TPC):
                sp.wait_ge(rows_ready, b + 1)
                sp.dma_start(out[b * CH:(b + 1) * CH].rearrange("(i p) n -> p i n", p=P),
                             base[:, b * TPC:(b + 1) * TPC]).then_inc(rows_stored, 16)
            sp.wait_ge(rows_stored, 16 * (TT // TPC))

        @block.gpsimd
        def _(pool):
            nc.gpsimd.memset(zeros[:], 0.0).then_inc(zeros_ready, 1)
            nc.gpsimd.memset(ident[:], 0.0).then_inc(consts2_ready, 1)
            nc.gpsimd.memset(ones_b[:], 1.0).then_inc(consts2_ready, 1)
            nc.gpsimd.memset(power[:], -0.5).then_inc(consts2_ready, 1)
            nc.gpsimd.memset(member[:, TT, :], 0.0).then_inc(consts2_ready, 1)
            pool.wait_ge(consts2_ready, 4)
            nc.gpsimd.affine_select(out=ident[:], in_=ident[:], compare_op=ALU.not_equal, fill=1.0, base=0,
                                    pattern=[[-1, P]], channel_multiplier=1).then_inc(consts2_ready, 1)
            nc.gpsimd.affine_select(out=before_b[:], in_=ones_b[:], compare_op=ALU.is_gt, fill=0.0, base=0,
                                    pattern=[[1, P]], channel_multiplier=-1).then_inc(consts2_ready, 1)
            pool.wait_ge(slots_ready, 1)
            pool.wait_ge(slots_cleared, 16 * ((SLOTS + 7) // 8))
            pool.wait_ge(x1_loaded, 16)
            for i in range(TT):
                for k in range(TOP_K):
                    pool.indirect_dma_start(out=slot_x, out_offset=bass.IndirectOffsetOnAxis(ap=slot[:, k, i:i + 1], axis=0),
                                            in_=x1[:, i, :], in_offset=None).then_inc(scattered, 16)

            def store(j, r, j0):
                pool.wait_ge(y_taken, j + (TT + 1))
                pool.dma_start(slot_y[bass.ds(j * P, P), :], ys[:, r, :]).then_inc(ys_stored[r], 16)

            over_slots(pool, store, SLOTS)
            for r in range(RING):
                pool.wait_ge(ys_stored[r], 16 * ((SLOTS - 1 - r) // RING + 1))

            def gather(b):
                if b >= 2:
                    pool.wait_ge(sums_ready, b - 1)
                for i in range(TPC):
                    for k in range(TOP_K):
                        pool.indirect_dma_start(
                            out=yg[:, b % 2, i, k, :], out_offset=None, in_=slot_y,
                            in_offset=bass.IndirectOffsetOnAxis(ap=slot[:, k, b * TPC + i:b * TPC + i + 1], axis=0))\
                            .then_inc(gathered[b % 2], 16)

            for b in range(TT // TPC + 1):
                if b < TT // TPC:
                    gather(b)
                if b:
                    pool.wait_ge(var2_ready, b)
                    nc.gpsimd.tensor_tensor(rstd[:], var_eps[:], power[:], ALU.pow).then_inc(rstd2_ready, 1)

        @block.scalar
        def _(act):
            for p in range(1, TT // 2, 2):
                act.wait_ge(pe_x1t, p + 1)
                nc.scalar.activation(x1_t[:, :, 2 * p * P:2 * (p + 1) * P].rearrange("p k (i n) -> p k i n", i=2),
                                     xt_ps[:, p % 2].rearrange("p (i k n) -> p k i n", i=2, k=KT), ACT.Copy)\
                  .then_inc(x1t_copied, 1)
            act.wait_ge(shift_ready, 1)
            nc.scalar.activation(probs[:], shifted[:], ACT.Exp).then_inc(exps_ready, 1)

            def gate_of(n, par, n0):
                act.wait_ge(pe_gu, n + 1)
                if n0 >= 2:
                    act.wait_ge(hidden_done, n - 1)
                nc.scalar.activation(silu[:, par], gu_ps[:, par, 0:INTER], ACT.Silu).then_inc(silu_done, 1)

            for n in range(SHARED):
                gate_of(n, n % 2, n)

            def slot_tile(j, r, j0):
                act.wait_ge(pe_xt, j + 1)
                if j0 >= 2:
                    act.wait_ge(pe_gu, j + (SHARED - 1))
                nc.scalar.activation(xg_t[:, j0 % 2], xt_ps[:, j0 % 2, 0:E].rearrange("p (k n) -> p k n", k=KT), ACT.Copy)\
                  .then_inc(xt_copied, 1)
                if j0:
                    gate_of(j + (SHARED - 1), (j0 + 1) % 2, SHARED)

            over_slots(act, slot_tile, SLOTS)
            gate_of(ITEMS - 1, (ITEMS - 1) % 2, SHARED)

        @block.tensor
        def _(pe):
            pe.wait_ge(consts2_ready, 6)
            pe.wait_ge(x1_loaded, 16)
            for p in range(TT // 2):
                if p >= 2:
                    pe.wait_ge(x1t_even if p % 2 == 0 else x1t_copied, p // 2)
                for i in range(2):
                    for k in range(KT):
                        last = nc.tensor.transpose(xt_ps[:, p % 2, (2 * i + k) * P:(2 * i + k + 1) * P],
                                                   x1[:, 2 * p + i, k * P:(k + 1) * P], ident[:])
                last.then_inc(pe_x1t, 1)
            pe.wait_ge(x1t_even, TT // 4)
            pe.wait_ge(x1t_copied, TT // 4)
            pe.wait_ge(small_loaded, 32)
            for i in range(TT):
                for k in range(KT):
                    last = nc.tensor.matmul(xt_ps[:, 0, i * EXPERTS:(i + 1) * EXPERTS], x1_t[:, k, i * P:(i + 1) * P],
                                            gate[:, k, :], start=(k == 0), stop=(k == KT - 1))
            last.then_inc(pe_logits, 1)

            def ranks():
                pe.wait_ge(members_ready, 1)
                r = xt_ps[:, 1, 0:(TT + 1) * EXPERTS].rearrange("p (i e) -> p i e", e=EXPERTS)
                nc.tensor.matmul(r, before_b[:], member[:], start=True, stop=False)
                for i in range(TT):
                    last = nc.tensor.matmul(r[:, i + 1:, :], ones_b[:],
                                            member[:, i:i + 1, :].to_broadcast([P, TT - i, EXPERTS]),
                                            start=False, stop=(i == TT - 1))
                last.then_inc(pe_ranks, 1)

            def up(n, par, n0, x_of, e):
                if n0 >= 2:
                    pe.wait_ge(hidden_done, n - 1)
                for k in range(KT):
                    last = nc.tensor.matmul(gu_ps[:, par, 0:2 * INTER], x_of(k), w_up[:, e, k, :],
                                            start=(k == 0), stop=(k == KT - 1))
                last.then_inc(pe_gu, 1)

            def turn_hidden(n, par, n0):
                pe.wait_ge(hidden_done, n + 1)
                if n0 >= 2:
                    pe.wait_ge(ht_copied, n - 1)
                for k in range(2):
                    last = nc.tensor.transpose(ht_ps[0:HALF, par, k * P:(k + 1) * P],
                                               hidden[:, par, k * HALF:(k + 1) * HALF], ident[:])
                last.then_inc(pe_ht, 1)

            def down(n, par, bank, group, e, start=True, stop=True):
                pe.wait_ge(ht_copied, n + 1)
                if start and group is not None:
                    pe.wait_ge(y_taken, group)
                for k in range(2):
                    last = nc.tensor.matmul(y_ps[:, bank, 0:E], hidden_t[:, par, k, :], w_dn[:, e, k, :],
                                            start=(start and k == 0), stop=(stop and k == 1))
                last.then_inc(pe_y, 1)

            def down_shared(n):
                i, half = divmod(n, 2)
                down(n, n % 2, i % 2, i - 1 if i >= 2 else None, EXPERTS + half, half == 0, half == 1)

            pe.wait_ge(shared_loaded, 32)
            for n in range(SHARED):
                i, half = divmod(n, 2)
                up(n, n % 2, n, lambda k: x1_t[:, k, i * P:(i + 1) * P], EXPERTS + half)
                if n >= 1:
                    turn_hidden(n - 1, (n - 1) % 2, n - 1)
                if n >= 2:
                    down_shared(n - 2)
                if n == RANKS_AT:
                    ranks()

            def turn_rows(j, r, par, j0):
                pe.wait_ge(xg_loaded[r], j_count(j, j0))
                if j0 >= 2:
                    pe.wait_ge(xt_copied, j - 1)
                for k in range(KT):
                    last = nc.tensor.transpose(xt_ps[:, par, k * P:(k + 1) * P], xg[:, r, k * P:(k + 1) * P], ident[:])
                last.then_inc(pe_xt, 1)

            def j_count(j, j0):
                return (j - j0) * (16 // RING) + 16 * (j0 // RING + 1)

            def expert_of(j):
                return pe.value_load(expert[0:1, bass.ds(j, 1)], min_val=0, max_val=EXPERTS - 1)

            def slot_tile(j, r, j0):
                if j0 == 0:
                    pe.wait_ge(experts_ready, 1)
                    pe.wait_ge(experts_loaded, 16 * 2 * 4)
                    pe.wait_ge(slots_ready, 1)
                    turn_rows(0, 0, 0, 0)
                if j0 + 1 < SLOTS:
                    turn_rows(j + 1, (r + 1) % RING, (j0 + 1) % 2, j0 + 1)
                pe.wait_ge(xt_copied, j + 1)
                up(j + SHARED, j0 % 2, SHARED, lambda k: xg_t[:, j0 % 2, k, :], bass.ds(expert_of(j), 1))
                turn_hidden(j + (SHARED - 1), (j0 + 1) % 2, SHARED)
                if j0 < 2:
                    down_shared(SHARED - 2 + j0)
                else:
                    down(j + (SHARED - 2), j0 % 2, (TT + j0) % 2, j + (TT - 3), bass.ds(expert_of(j - 2), 1))

            over_slots(pe, slot_tile, SLOTS)
            turn_hidden(ITEMS - 1, (ITEMS - 1) % 2, SHARED)
            for j in range(SLOTS - 2, SLOTS):
                down(j + SHARED, j % 2, (TT + j) % 2, j + TT - 1, bass.ds(expert_of(j), 1))

        @block.vector
        def _(dve):
            chain = [0]

            def link(ins):
                chain[0] += 1
                ins.then_inc(chain_sem, 1)
                dve.wait_ge(chain_sem, chain[0])

            for p in range(0, TT // 2, 2):
                dve.wait_ge(pe_x1t, p + 1)
                nc.vector.tensor_copy(x1_t[:, :, 2 * p * P:2 * (p + 1) * P].rearrange("p k (i n) -> p k i n", i=2),
                                      xt_ps[:, p % 2].rearrange("p (i k n) -> p k i n", i=2, k=KT))\
                  .then_inc(x1t_even, 1)

            def along_e(v):
                return v.unsqueeze(2).to_broadcast([P, TT, EXPERTS])

            def softmax():
                dve.wait_ge(pe_logits, 1)
                dve.wait_ge(small_loaded, 32)
                logits = xt_ps[:, 0, 0:TT * EXPERTS].rearrange("p (i e) -> p i e", e=EXPERTS)
                link(nc.vector.tensor_reduce(row[:, 0, :], logits, AX.X, ALU.max))
                nc.vector.tensor_tensor(shifted[:], logits, along_e(row[:, 0, :]), ALU.subtract).then_inc(shift_ready, 1)

            def scale_probs():
                dve.wait_ge(exps_ready, 1)
                link(nc.vector.tensor_reduce(row[:, 1, :], probs[:], AX.X, ALU.add))
                link(nc.vector.reciprocal(row[:, 2, :], row[:, 1, :]))
                link(nc.vector.tensor_tensor(shifted[:], probs[:], along_e(row[:, 2, :]), ALU.mult))

            def top_two(tiles_of):
                for i in tiles_of:
                    link(nc.vector.max(best[:, i, :], shifted[:, i, :]))
                    last = nc.vector.max_index(best_at[:, i, :], best[:, i, :], shifted[:, i, :])
                link(last)

            def memberships():
                link(nc.vector.tensor_copy(best_f[:].rearrange("p k i -> p i k"), best_at[:, :, 0:TOP_K]))
                for k in range(TOP_K):
                    link(nc.vector.tensor_tensor(chosen[:, k], iota_e.unsqueeze(1).to_broadcast([P, TT, EXPERTS]),
                                                 along_e(best_f[:, k, :]), ALU.is_equal))
                dve.wait_ge(consts2_ready, 6)
                nc.vector.tensor_tensor(member[:, 0:TT, :], chosen[:, 0], chosen[:, 1], ALU.add).then_inc(members_ready, 1)

            def slots_of():
                dve.wait_ge(pe_ranks, 1)
                r = xt_ps[:, 1, 0:(TT + 1) * EXPERTS].rearrange("p (i e) -> p i e", e=EXPERTS)
                link(nc.vector.tensor_copy(count[:], r[:, TT, :]))
                link(nc.vector.tensor_tensor(grid[:], count[:].unsqueeze(2).to_broadcast([P, EXPERTS, TT]),
                                             step_128.unsqueeze(1).to_broadcast([P, EXPERTS, TT]), ALU.is_gt))
                link(nc.vector.tensor_reduce(tiles[:, 0, :], grid[:], AX.X, ALU.add))
                link(nc.vector.tensor_tensor(grid[:], tiles[:, 0:1, :].to_broadcast([P, EXPERTS, EXPERTS]), earlier, ALU.mult))
                link(nc.vector.tensor_reduce(tiles[:, 1, :], grid[:], AX.X, ALU.add))
                link(nc.vector.tensor_scalar(count[:], tiles[:, 1, :], float(P), None, ALU.mult))
                link(nc.vector.tensor_tensor(place[:], r[:, 0:TT, :], count[:].unsqueeze(1).to_broadcast([P, TT, EXPERTS]), ALU.add))
                for k in range(TOP_K):
                    link(nc.vector.tensor_tensor(place_of[:], place[:], chosen[:, k], ALU.mult))
                    link(nc.vector.tensor_reduce(slot_f[:, k, :], place_of[:], AX.X, ALU.add))
                nc.vector.tensor_copy(slot[:], slot_f[:]).then_inc(slots_ready, 1)

            def experts_of():
                link(nc.vector.tensor_tensor(tiles[:, 2, :], tiles[:, 0, :], tiles[:, 1, :], ALU.add))
                link(nc.vector.tensor_tensor(grid2[:], tiles[:, 2:3, :].to_broadcast([P, 48, EXPERTS]),
                                             iota_slot.unsqueeze(2).to_broadcast([P, 48, EXPERTS]), ALU.is_le))
                link(nc.vector.tensor_reduce(expert_f[:], grid2[:], AX.X, ALU.add))
                nc.vector.tensor_scalar(expert[:], expert_f[:], float(EXPERTS - 1), None, ALU.min).then_inc(experts_ready, 1)

            def hide(n, par, n0):
                dve.wait_ge(silu_done, n + 1)
                if n0 >= 2:
                    dve.wait_ge(pe_ht, n - 1)
                nc.vector.tensor_tensor(hidden[:, par], silu[:, par], gu_ps[:, par, INTER:2 * INTER], ALU.mult)\
                  .then_inc(hidden_done, 1)

            def copy_hidden(n, par, n0):
                dve.wait_ge(pe_ht, n + 1)
                if n0 >= 2:
                    dve.wait_ge(pe_y, n - 1)
                nc.vector.tensor_copy(hidden_t[:, par], ht_ps[0:HALF, par, 0:2 * P].rearrange("p (k n) -> p k n", k=2))\
                  .then_inc(ht_copied, 1)

            def take_shared(i):
                dve.wait_ge(pe_y, 2 * i + 2)
                nc.vector.tensor_tensor(base[:, i, :], x1[:, i, :], y_ps[:, i % 2, 0:E], ALU.add).then_inc(y_taken, 1)

            stages = {0: softmax, 1: scale_probs, 2: lambda: top_two(range(0, 4)), 3: lambda: top_two(range(4, 8)),
                      4: lambda: top_two(range(8, 12)), 5: lambda: top_two(range(12, 16)), 6: memberships,
                      RANKS_AT + 1: slots_of, RANKS_AT + 2: experts_of}
            dve.wait_ge(x1_loaded, 16)
            softmax()
            for n in range(SHARED):
                if n in stages and n:
                    stages[n]()
                hide(n, n % 2, n)
                if n >= 1:
                    copy_hidden(n - 1, (n - 1) % 2, n - 1)
                if n >= 3 and n % 2:
                    take_shared((n - 3) // 2)

            def take(j, r, j0):
                if j0 >= RING:
                    dve.wait_ge(ys_stored[r], (j - j0) * (16 // RING) + 16 * (j0 // RING))
                dve.wait_ge(pe_y, j + (SHARED + 1))
                nc.vector.tensor_copy(ys[:, r, :], y_ps[:, (TT + j0) % 2, 0:E]).then_inc(y_taken, 1)

            def slot_tile(j, r, j0):
                hide(j + SHARED, j0 % 2, SHARED)
                copy_hidden(j + (SHARED - 1), (j0 + 1) % 2, SHARED)
                if j0 < 2:
                    if j0 == 1:
                        take_shared(TT - 1)
                else:
                    take(j - 2, (r + 2) % RING, j0 - 2)

            over_slots(dve, slot_tile, SLOTS)
            copy_hidden(ITEMS - 1, (ITEMS - 1) % 2, SHARED)
            for j in range(SLOTS - 2, SLOTS):
                take(j, j % RING, j)

            for b in range(TT // TPC):
                if b:
                    dve.wait_ge(rows_ready, b)
                dve.wait_ge(gathered[b % 2], 16 * TPC * TOP_K * (b // 2 + 1))
                for i in range(TPC):
                    at = b * TPC + i
                    for k in range(TOP_K):
                        last = nc.vector.scalar_tensor_tensor(
                            out=base[:, at, :], in0=yg[:, b % 2, i, k, :], scalar=best[:, at, k:k + 1],
                            in1=base[:, at, :], op0=ALU.mult, op1=ALU.add)
                        if (i, k) != (TPC - 1, TOP_K - 1):
                            link(last)
                last.then_inc(sums_ready, 1)
                dve.wait_ge(sums_ready, b + 1)
                for i in range(TPC):
                    last = nc.vector.bn_stats(stats[:, i, :], base[:, b * TPC + i, :])
                link(last)
                for i in range(TPC):
                    last = nc.vector.bn_aggr(mean_var[:, i, :], stats[:, i, :])
                link(last)
                nc.vector.tensor_scalar(var_eps[:], mean_var[:, :, 1], EPS, None, ALU.add).then_inc(var2_ready, 1)
                dve.wait_ge(rstd2_ready, b + 1)
                for i in range(TPC):
                    at = b * TPC + i
                    last = nc.vector.tensor_scalar(base[:, at, :], base[:, at, :], mean_var[:, i, 0:1],
                                                   rstd[:, i:i + 1], ALU.subtract, ALU.mult)
                last.then_inc(rows_ready, 1)


def build_program(nc, t, out):
    x1_dram = nc.dram_tensor("x1_rows", out.shape, F32, kind="Internal").ap()
    build_attention(nc, t, x1_dram)
    build_experts(nc, t, x1_dram, out)


def layout(inputs):
    a = {k.removeprefix("L0_"): np.asarray(v) for k, v in inputs.items()}
    x = a["attn_x"][0]
    S = x.shape[0]
    even, odd = list(range(NOPE, DH, 2)), list(range(NOPE + 1, DH, 2))
    own = list(range(NOPE)) + even + odd
    partner = list(range(NOPE)) + odd + even
    cols = [h * DH + d for order in (own, partner) for h in range(HEADS) for d in order]
    freqs = np.float32(1.0) / np.float32(THETA) ** (np.arange(0, ROPE_D, 2, dtype=np.float32) / np.float32(ROPE_D))
    angle = np.arange(S, dtype=np.float32)[:, None] * freqs[None, :]
    cos, sin = np.cos(angle).T, np.sin(angle).T
    head = np.zeros((2, DH, S), np.float32)
    head[0, :NOPE] = 1.0
    head[0, NOPE:] = np.concatenate([cos, cos])
    head[1, NOPE:] = np.concatenate([-sin, sin])
    w1, w2, w3 = (a[f"ffn_w{n}"] for n in (1, 2, 3))
    s1, s3 = (a[f"ffn_sw{n}"].reshape(2, INTER, -1) for n in (1, 3))
    s2 = a["ffn_sw2"].reshape(-1, 2, INTER).transpose(1, 0, 2)
    up = np.concatenate([np.concatenate([w1, s1]), np.concatenate([w3, s3])], axis=1).transpose(0, 2, 1)
    down = np.concatenate([w2, s2]).transpose(0, 2, 1)
    n16 = np.arange(EXPERTS, dtype=np.float32)
    consts = np.concatenate([n16, n16 * P, (n16[None, :] < n16[:, None]).astype(np.float32).ravel(),
                             np.arange(48, dtype=np.float32)])
    consts = np.ascontiguousarray(np.broadcast_to(consts, (P, consts.size)))
    c = np.ascontiguousarray
    return {
        "x": c(x), "xT": c(x.T),
        "w_q": c(a["attn_Wq"][:, cols]),
        "w_down": c(np.concatenate([a["attn_Wkv_down"]] * 2, axis=1)),
        "w_k": c(np.concatenate([a["attn_Wk_up"][:, cols]] * 2, axis=0)),
        "w_v": c(np.concatenate([a["attn_Wv_up"]] * 2, axis=0)),
        "gate": c(a["ffn_gate_w"].T.reshape(2, P, EXPERTS).transpose(1, 0, 2)),
        "w_up": c(up.reshape(EXPERTS + 2, 2, P, 2 * INTER).transpose(2, 0, 1, 3)),
        "w_dn": c(down.reshape(EXPERTS + 2, 2, HALF, 256).transpose(2, 0, 1, 3)),
        "consts": consts,
        "rope": c(np.concatenate([head] * (P // DH), axis=1).transpose(1, 0, 2)),
    }


def kernel(**inputs):
    from concourse import bacc
    from concourse.bass_utils import run_bass_kernel_spmd

    arrays = layout(inputs)
    S, E = arrays["x"].shape
    nc = bacc.Bacc("TRN2", target_bir_lowering=False, num_devices=1)
    t = {name: nc.dram_tensor(name, a.shape, mybir.dt.from_np(a.dtype), kind="ExternalInput").ap()
         for name, a in arrays.items()}
    out = nc.dram_tensor("out", (S, E), F32, kind="ExternalOutput").ap()
    build_program(nc, t, out)
    got = run_bass_kernel_spmd(nc, [arrays], core_ids=[0]).results[0]["out"]
    return got.reshape(1, S, E)
```

```python
from contextlib import ExitStack

import numpy as np

import concourse.bass as bass
from concourse import mybir

F32 = mybir.dt.float32
F32R = mybir.dt.float32r
BF16 = mybir.dt.bfloat16
I32 = mybir.dt.int32
U32 = mybir.dt.uint32
ALU = mybir.AluOpType
ACT = mybir.ActivationFunctionType
AX = mybir.AxisListType

P = 128
HEADS, DH, LATENT = 16, 16, 64
NOPE = DH // 4
ROPE_D = DH - NOPE
THETA = 10000.0
EPS = 1e-5
CH = 512
TPC = CH // P
GH = 4
UNITS_PER_CHUNK = HEADS // GH
SPLIT = 3 * DH
STACK = 2 * SPLIT
ROWS = STACK + 2
NEG = -3.0e38
BANKS_A_STEP = (5.59, 5.04, 4.58, 4.19)
MAX_AHEAD = 3
JOBS_A_STEP = 1
ROPE_AHEAD = 8
SCORE_BANKS = 3
MAX_BANKS = 3
RAW_BUFS = 3


def build_attention(nc, t, x1_dram):
    S, E = t["x"].shape
    NCH = S // CH
    UNITS = NCH * UNITS_PER_CHUNK
    KT = E // P
    SCALE = 1.0 / float(np.sqrt(DH))

    steps = [(u, b) for u in range(UNITS) for b in range(TPC * (u // UNITS_PER_CHUNK + 1))]
    first_step = {}
    for s, (u, b) in enumerate(steps):
        first_step.setdefault(u, s)
    first_step[UNITS] = len(steps)

    def max_banks(u):
        c = u // UNITS_PER_CHUNK
        return [(u, h, i, kb) for h in range(GH) for i in range(TPC) for kb in range(c + 1)]

    def projection_jobs(c):
        return [("latent", c, 0), ("rope", c, 0), ("rope", c, 1), ("rope", c, 2), ("rope", c, 3),
                ("value", c, 0), ("value", c, 1), ("rope", c, 4), ("rope", c, 5), ("rope", c, 6), ("rope", c, 7)]

    NS = len(steps)
    END = NS + 6
    max_at = {s: [] for s in range(-1, END)}
    aux_at = {s: [] for s in range(-1, END)}
    filled = [0.0]
    for u, b in steps:
        filled.append(filled[-1] + BANKS_A_STEP[u // UNITS_PER_CHUNK])

    def room(s):
        return int(filled[s + 1]) - int(filled[s])

    at = NS
    for u in reversed(range(UNITS)):
        at = min(at, first_step[u] - MAX_AHEAD)
        for bank in reversed(max_banks(u)):
            while at >= 0 and len(max_at[at]) >= room(at):
                at -= 1
            at = max(at, -1)
            max_at[at].insert(0, bank)
    last_bank_at = {u: max(s for s in max_at for m in max_at[s] if m[0] == u) for u in range(UNITS)}
    first_bank_at = {u: min(s for s in max_at for m in max_at[s] if m[0] == u) for u in range(UNITS)}
    at = NS
    for c in reversed(range(NCH)):
        for job in reversed(projection_jobs(c)):
            if job[0] != "value":
                at = min(at, first_bank_at[c * UNITS_PER_CHUNK + (2 if job[0] == "rope" and job[2] >= 4 else 0)] - ROPE_AHEAD)
            at = min(at, first_step[c * UNITS_PER_CHUNK] - 2)
            while at >= 0 and len(aux_at[at]) >= JOBS_A_STEP:
                at -= 1
            at = max(at, -1)
            aux_at[at].insert(0, job)
    for u in range(UNITS):
        after = last_bank_at[u] + 1 if last_bank_at[u] >= 0 else -1
        aux_at[after].insert(0, ("maxima", u)) if after >= 0 else aux_at[after].append(("maxima", u))
        aux_at[first_step[u + 1] + 2].append(("out", u))
    aux_at[-1].remove(("maxima", 0))
    aux_at[-1].insert(len(projection_jobs(0)), ("maxima", 0))
    q_load_at = {}
    for u in range(4, UNITS):
        c, g = divmod(u, UNITS_PER_CHUNK)
        projected = next(s for s in aux_at if ("rope", c, 4 * (g // 2) + 3) in aux_at[s])
        q_load_at[u] = max(first_step[u - 3], projected + 1)
        assert first_bank_at[u] > q_load_at[u], u
    norm_at = {first_step[(c + 1) * UNITS_PER_CHUNK] + 3: c for c in range(NCH)}

    aux_order = [j for s in range(-1, END) for j in aux_at[s]]
    aux_no = {j: n + 1 for n, j in enumerate(aux_order)}
    prologue = aux_at[-1]
    by_act = {j: n + 1 for n, j in enumerate(j for j in aux_order if j[0] in ("rope", "value"))}
    by_dve = {j: n + 1 for n, j in enumerate(j for j in aux_order if j[0] not in ("rope", "value"))}
    max_order = [m for s in range(-1, END) for m in max_at[s]]
    max_no = {m: n + 1 for n, m in enumerate(max_order)}
    diag_before = [0]
    for u, b in steps:
        diag_before.append(diag_before[-1] + (b >= TPC * (u // UNITS_PER_CHUNK)))

    def quarters(items, n=4):
        return [items[len(items) * k // n:len(items) * (k + 1) // n] for k in range(n)]

    kq_dram = nc.dram_tensor("kq_split", (NCH, 4, 2, 3, DH * GH, CH), F32, kind="Internal").ap()

    with ExitStack() as ctx:
        def sb(name, shape, dt=F32):
            return ctx.enter_context(nc.sbuf_tensor(name, shape, dt))

        def ps(name, shape):
            return ctx.enter_context(nc.psum_tensor(name, shape, F32))

        def sem(name):
            return ctx.enter_context(nc.semaphore(name))

        k_stack = sb("k_stack", [ROWS, HEADS // 2, S], F32R)
        q_stack = sb("q_stack", [ROWS, 4, GH, CH], F32R)
        v_ones = sb("v_ones", [P, S // P, HEADS, DH + 1])
        probs = sb("probs", [P, 2, GH, CH])
        w_raw = sb("w_raw", [P, 2048])
        w_split = sb("w_split", [P, 2, 2048], F32R)
        x_raw = sb("x_raw", [P, KT, CH])
        x_split = sb("x_split", [P, 2, KT, CH], F32R)
        rope = sb("rope_sb", [P, 2, CH])
        latent = sb("latent", [P, CH], F32R)
        latent_hi = sb("latent_hi", [P, CH], F32R)
        rope_raw = sb("rope_raw", [P, RAW_BUFS, CH])
        by_cos = sb("by_cos", [P, 256])
        by_sin = sb("by_sin", [P, 256])
        roped = sb("roped", [P, 2, 256])
        kq_stage = sb("kq_stage", [P, 2, 2, CH], F32R)
        ident = sb("ident", [P, P])
        ident_b = sb("ident_b", [P, P], BF16)
        mask_b = sb("mask_b", [P, P], BF16)
        mx = sb("mx", [P, 2, GH * TPC, 4])
        mx_row = sb("mx_row", [P, 2, GH * TPC])
        m_rows = sb("m_rows", [GH * TPC, 2, 2, P], F32R)
        out_t = sb("out_t", [P, CH])
        recip = sb("recip", [P, TPC, GH])
        attn = sb("attn", [P, TPC, E])
        x_tok = w_raw[:, 0:TPC * E].rearrange("p (i n) -> p i n", i=TPC)
        summed = w_raw[:, TPC * E:2 * TPC * E].rearrange("p (i n) -> p i n", i=TPC)
        stats = sb("stats", [P, TPC, 6])
        mean_var = sb("mean_var", [P, TPC, 2])
        power = sb("power", [P, TPC])
        var_eps = sb("var_eps", [P, TPC])
        rstd = sb("rstd", [P, TPC])

        scores = ps("scores", [P, SCORE_BANKS, CH])
        max_ps = ps("max_ps", [P, MAX_BANKS, CH])
        pv_ps = ps("pv_ps", [P, CH])
        aux_ps = ps("aux_ps", [P, CH])

        OFF_Q, OFF_D, OFF_K, OFF_V = 0, 1024, 1280, 1792
        wq = w_split[:, :, OFF_Q:OFF_D].rearrange("p s (k n) -> p s k n", k=KT)
        wd = w_split[:, :, OFF_D:OFF_K].rearrange("p s (k n) -> p s k n", k=KT)
        wk = w_split[:, :, OFF_K:OFF_V]
        wv = w_split[:, :, OFF_V:2048]

        w_loaded = [sem(f"w_loaded{n}") for n in range(3)]
        hi_ready = sem("hi_ready")
        x_loaded = sem("x_loaded")
        rope_loaded = sem("rope_loaded")
        tok_loaded = sem("tok_loaded")
        kq_stored = sem("kq_stored")
        k_stacked = sem("k_stacked")
        q_stacked = sem("q_stacked")
        m_stacked = sem("m_stacked")
        consts_ready = sem("consts_ready")
        dve_consts = sem("dve_consts")
        zeros_low = sem("zeros_low")
        zeros_high = sem("zeros_high")
        ones_first = sem("ones_first")
        ones_ready = sem("ones_ready")
        w_ready = sem("w_ready")
        x_ready = sem("x_ready")
        pe_scores = sem("pe_scores")
        pe_max = sem("pe_max")
        pe_pv = sem("pe_pv")
        pe_aux = sem("pe_aux")
        exp_done = sem("exp_done")
        mask_done = sem("mask_done")
        max_done = sem("max_done")
        act_read = sem("act_read")
        dve_read = sem("dve_read")
        roped_ready = sem("roped_ready")
        kq_ready = sem("kq_ready")
        mx_ready = sem("mx_ready")
        pv_done = sem("pv_done")
        dve_chain = sem("dve_chain")
        pool_chain = sem("pool_chain")
        var_ready = sem("var_ready")
        rstd_ready = sem("rstd_ready")
        x1_ready = sem("x1_ready")
        x1_stored = sem("x1_stored")

        block = ctx.enter_context(nc.Block())

        def in_second(n):
            return n <= len(prologue) and n % 2 == 0

        def aux_bank(job):
            return scores[:, SCORE_BANKS - 1] if in_second(aux_no[job]) else aux_ps[:]

        def wait_read(eng, job):
            if job in by_act:
                eng.wait_ge(act_read, by_act[job])
            else:
                eng.wait_ge(dve_read, by_dve[job])

        def rotate(eng, op, job, link):
            c, n = job[1:]
            k = 8 * c + n
            cols = slice(256 * (n % 2), 256 * (n % 2) + 256)
            if n == 0:
                eng.wait_ge(rope_loaded, 16 * (c + 1))
            eng.wait_ge(act_read, by_act[job])
            if k:
                eng.wait_ge(roped_ready, k)
            link(op.tensor_tensor(by_cos[:], rope_raw[:, k % RAW_BUFS, 0:256], rope[:, 0, cols], ALU.mult))
            link(op.tensor_tensor(by_sin[:], rope_raw[:, k % RAW_BUFS, 256:512], rope[:, 1, cols], ALU.mult))
            if k >= 2:
                eng.wait_ge(kq_ready, k - 1)
            op.tensor_tensor(roped[:, k % 2], by_cos[:], by_sin[:], ALU.add).then_inc(roped_ready, 1)

        @block.sync
        def _(sp):
            sp.dma_start(x_raw[:], t["xT"][:, 0:CH].rearrange("(k p) n -> p k n", p=P)).then_inc(x_loaded, 16)
            sp.dma_start(rope[:], t["rope"][:, :, 0:CH]).then_inc(rope_loaded, 16)
            def load_q(u):
                c, g = divmod(u, UNITS_PER_CHUNK)
                m, j0 = g // 2, GH * (g % 2)
                if u == 0:
                    sp.wait_ge(zeros_low, 1)
                if u == 2:
                    sp.wait_ge(zeros_high, 1)
                if u:
                    sp.wait_ge(q_stacked, 16 * 2 * u)
                if u >= 4:
                    sp.wait_ge(pe_scores, GH * first_step[u - 3])
                for par in range(2):
                    src = kq_dram[c, 2 * m + 1, par].rearrange("copy (d j) n -> (copy d) j n", j=GH)
                    sp.dma_start(q_stack[par * SPLIT:(par + 1) * SPLIT, u % 4, par::2, :].bitcast(F32),
                                 src[:, j0 // 2:j0 // 2 + 2, :]).then_inc(q_stacked, 16)

            def load_chunk(c):
                sp.wait_ge(x_ready, c)
                sp.dma_start(x_raw[:], t["xT"][:, c * CH:(c + 1) * CH].rearrange("(k p) n -> p k n", p=P))\
                    .then_inc(x_loaded, 16)

            def load_tables(c):
                sp.wait_ge(roped_ready, 8 * c)
                sp.dma_start(rope[:], t["rope"][:, :, c * CH:(c + 1) * CH]).then_inc(rope_loaded, 16)

            def store_piece(c, n):
                piece = 4 * c + n
                m, is_q = n // 2, n % 2
                sp.wait_ge(kq_ready, 2 * (piece + 1))
                for copy, part in enumerate((0, 1, 0) if is_q else (0, 0, 1)):
                    sp.dma_start(kq_dram[c, n, :, copy], kq_stage[:, piece % 2, part].bitcast(F32)).then_inc(kq_stored, 16)
                sp.wait_ge(kq_stored, 16 * 3 * (piece + 1))
                if not is_q:
                    if piece:
                        sp.wait_ge(k_stacked, 16 * (piece // 2))
                    sp.dma_start(k_stack[0:STACK, 4 * m:4 * m + 4, c * CH:(c + 1) * CH].bitcast(F32),
                                 kq_dram[c, n].rearrange("two copy (d j) n -> (two copy d) j n", j=GH)).then_inc(k_stacked, 16)

            for s in range(-1, END):
                for job in aux_at[s]:
                    if job[0] == "rope" and job[2] % 2:
                        store_piece(job[1], job[2] // 2)
                        if job[1] == 0 and job[2] % 4 == 3:
                            load_q(job[2] // 4 * 2)
                            load_q(job[2] // 4 * 2 + 1)
                        if job[2] == 1 and job[1] + 1 < NCH:
                            load_chunk(job[1] + 1)
                        if job[2] == 7 and job[1] + 1 < NCH:
                            load_tables(job[1] + 1)
                for u in range(4, UNITS):
                    if q_load_at[u] == s:
                        load_q(u)
            sp.wait_ge(x1_stored, 16 * NCH)

        @block.gpsimd
        def _(pool):
            chain = [0]

            def link(ins):
                chain[0] += 1
                ins.then_inc(pool_chain, 1)
                pool.wait_ge(pool_chain, chain[0])

            def split(hi, lo, src, done):
                link(nc.gpsimd.tensor_scalar(hi, src, 1.0, 0.0, ALU.mult, ALU.add))
                nc.gpsimd.tensor_tensor(lo, src, hi.bitcast(F32), ALU.subtract).then_inc(done, 1)

            def split_x(c):
                pool.wait_ge(x_loaded, 16 * (c + 1))
                pool.wait_ge(pe_aux, aux_no[("rope", c - 1, 7)])
                split(x_split[:, 0], x_split[:, 1], x_raw[:], x_ready)
                pool.wait_ge(x_ready, c + 1)

            def load_tokens(c):
                pool.dma_start(x_tok[:], t["x"][c * CH:(c + 1) * CH, :].rearrange("(i p) n -> p i n", p=P))\
                    .then_inc(tok_loaded, 16)

            nc.gpsimd.memset(q_stack[0:STACK, 0:2].bitcast(F32), 0.0).then_inc(zeros_low, 1)
            link(nc.gpsimd.memset(k_stack[STACK:ROWS, :, 0:CH].bitcast(F32), 1.0))
            link(nc.gpsimd.memset(ident[:], 0.0))
            link(nc.gpsimd.affine_select(out=ident[:], in_=ident[:], compare_op=ALU.not_equal, fill=1.0, base=0,
                                         pattern=[[-1, P]], channel_multiplier=1))
            nc.gpsimd.tensor_copy(ident_b[:], ident[:]).then_inc(consts_ready, 1)
            link(nc.gpsimd.memset(mask_b[:], 0.0))
            nc.gpsimd.affine_select(out=mask_b[:], in_=mask_b[:], compare_op=ALU.is_ge, fill=NEG, base=0,
                                    pattern=[[-1, P]], channel_multiplier=1).then_inc(consts_ready, 1)
            link(nc.gpsimd.memset(power[:], -0.5))

            def split_rope(c, n):
                k = 8 * c + n
                if c:
                    rotate(pool, nc.gpsimd, ("rope", c, n), link)
                pool.wait_ge(roped_ready, k + 1)
                piece = k // 2
                if piece >= 2 and n % 2 == 0:
                    pool.wait_ge(kq_stored, 16 * 3 * (piece - 1))
                cols = slice(256 * (n % 2), 256 * (n % 2) + 256)
                split(kq_stage[:, piece % 2, 0, cols], kq_stage[:, piece % 2, 1, cols], roped[:, k % 2], kq_ready)

            def inverse_deviation(c):
                pool.wait_ge(var_ready, c + 1)
                nc.gpsimd.tensor_tensor(rstd[:], var_eps[:], power[:], ALU.pow).then_inc(rstd_ready, 1)
                pool.wait_ge(x1_ready, c + 1)
                pool.dma_start(x1_dram[c * CH:(c + 1) * CH, :].rearrange("(i p) n -> p i n", p=P), summed[:])\
                    .then_inc(x1_stored, 16)
                if c + 1 < NCH:
                    load_tokens(c + 1)

            def split_jobs(jobs):
                for job in jobs:
                    if job[0] == "rope":
                        split_rope(job[1], job[2])
                    if job[0] == "rope" and job[2] == 7 and job[1] + 1 < NCH:
                        c = job[1] + 1
                        split_x(c)
                        nc.gpsimd.memset(k_stack[STACK:ROWS, :, c * CH:(c + 1) * CH].bitcast(F32), 1.0)\
                            .then_inc(ones_ready, 1)
                        pool.wait_ge(ones_ready, c)

            def mask(s):
                u, b = steps[s]
                c = u // UNITS_PER_CHUNK
                if b < TPC * c:
                    return
                off = P * (b - TPC * c)
                pool.wait_ge(exp_done, GH * (s + 1))
                v = probs[:, s % 2, :, off:off + P]
                nc.gpsimd.affine_select(out=v, in_=v, compare_op=ALU.is_ge, fill=0.0, base=0,
                                        pattern=[[0, GH], [1, P]], channel_multiplier=-1).then_inc(mask_done, 1)

            split_jobs(aux_at[-1])
            pool.wait_ge(w_ready, 3)
            load_tokens(0)
            for s in range(END):
                if s < NS:
                    mask(s)
                if s:
                    split_jobs(aux_at[s - 1])
                if s in norm_at:
                    inverse_deviation(norm_at[s])

        @block.scalar
        def _(act):
            act.dma_start(w_raw[:, OFF_D:OFF_K].rearrange("p (k n) -> p k n", k=KT),
                         t["w_down"].rearrange("(k p) n -> p k n", p=P)).then_inc(w_loaded[0], 16)
            act.dma_start(w_raw[:, OFF_K:OFF_V], t["w_k"]).then_inc(w_loaded[1], 16)
            act.dma_start(w_raw[:, OFF_V:2048], t["w_v"]).then_inc(w_loaded[1], 16)
            act.dma_start(w_raw[:, OFF_Q:OFF_D].rearrange("p (k n) -> p k n", k=KT),
                         t["w_q"].rearrange("(k p) n -> p k n", p=P)).then_inc(w_loaded[2], 16)
            act.wait_ge(x_loaded, 16)
            nc.scalar.activation(x_split[:, 0], x_raw[:], ACT.Copy).then_inc(hi_ready, 1)
            for n, (lo, hi, full) in enumerate(((OFF_D, OFF_K, 16), (OFF_K, 2048, 32), (OFF_Q, OFF_D, 16))):
                act.wait_ge(w_loaded[n], full)
                nc.scalar.activation(w_split[:, 0, lo:hi], w_raw[:, lo:hi], ACT.Copy).then_inc(hi_ready, 1)

            def store_maxima(u):
                wait_read(act, ("maxima", u))
                if u:
                    act.wait_ge(m_stacked, 32 * u)
                for part in range(2):
                    act.dma_start(q_stack[STACK + part:STACK + part + 1, u % 4].rearrange("o h n -> o (h n)").bitcast(F32),
                                  m_rows[:, u % 2, part, :].bitcast(F32)).then_inc(m_stacked, 16)

            def read_aux(job):
                kind, c, n = job
                act.wait_ge(pe_aux, aux_no[job])
                if kind == "rope":
                    k = 8 * c + n
                    if k >= RAW_BUFS:
                        act.wait_ge(roped_ready, k - RAW_BUFS + 1)
                    nc.scalar.activation(rope_raw[:, k % RAW_BUFS], aux_bank(job), ACT.Copy,
                                         scale=SCALE if (n // 2) % 2 else 1.0).then_inc(act_read, 1)
                else:
                    nc.scalar.activation(v_ones[:, TPC * c + 2 * n:TPC * c + 2 * n + 2, :, 0:DH],
                                         aux_bank(job).rearrange("p (t h d) -> p t h d", t=2, h=HEADS), ACT.Copy)\
                      .then_inc(act_read, 1)

            def run_jobs(jobs):
                for job in jobs:
                    if job in by_act:
                        read_aux(job)
                    elif job[0] == "maxima":
                        store_maxima(job[1])

            def copy_output(u):
                act.wait_ge(pe_pv, first_step[u + 1])
                if u:
                    act.wait_ge(pe_aux, aux_no[("out", u - 1)])
                nc.scalar.activation(out_t[:], pv_ps[:], ACT.Copy).then_inc(pv_done, 1)

            run_jobs(aux_at[-1])
            for s in range(END):
                jobs = quarters(aux_at[s], 2)
                if s < NS:
                    u, b = steps[s]
                    off = max(0, P * (b - TPC * (u // UNITS_PER_CHUNK)))
                for h in range(GH):
                    if s < NS:
                        n = GH * s + h
                        act.wait_ge(pe_scores, n + 1)
                        if s >= 2:
                            act.wait_ge(pe_pv, s - 1)
                        nc.scalar.activation(probs[:, s % 2, h, off:CH], scores[:, n % SCORE_BANKS, off:CH], ACT.Exp)\
                          .then_inc(exp_done, 1)
                    if h % 2:
                        run_jobs(jobs[h // 2])
                if s == NS or (s and s < NS and steps[s][1] == 0):
                    copy_output(steps[s - 1][0])

        @block.tensor
        def _(pe):
            def aux_free(job):
                n = aux_no[job]
                before = [m for m in range(1, n) if in_second(m) == in_second(n)]
                if before:
                    wait_read(pe, aux_order[before[-1] - 1])
                return aux_bank(job)

            def projection(job):
                kind, c, n = job
                if kind == "latent":
                    pe.wait_ge(x_ready, c + 1)
                    if c == 0:
                        pe.wait_ge(w_ready, 1)
                    aux = aux_free(job)
                    k = 0
                    for kt in range(KT):
                        for a, b in ((0, 0), (0, 1), (1, 0)):
                            last = nc.tensor.matmul(aux, wd[:, a, kt, :], x_split[:, b, kt, :],
                                                    start=(k == 0), stop=(k == 3 * KT - 1))
                            k += 1
                    last.then_inc(pe_aux, 1)
                elif kind == "rope":
                    piece, half = n // 2, n % 2
                    m, is_q = piece // 2, piece % 2
                    cols = slice(256 * half, 256 * half + 256)
                    if n == 0:
                        wait_read(pe, ("latent", c, 0))
                    if c == 0 and n < 3:
                        pe.wait_ge(w_ready, 3 if n == 2 else 2)
                    aux = aux_free(job)
                    for partner in range(2):
                        dst = aux[:, 256 * partner:256 * partner + 256]
                        w0 = 256 * partner + P * m
                        if is_q:
                            k = 0
                            for kt in range(KT):
                                for a, b in ((0, 0), (0, 1), (1, 0)):
                                    last = nc.tensor.matmul(dst, wq[:, a, kt, w0:w0 + P], x_split[:, b, kt, cols],
                                                            start=(k == 0), stop=(k == 3 * KT - 1))
                                    k += 1
                        else:
                            for a in range(2):
                                last = nc.tensor.matmul(dst, wk[:, a, w0:w0 + P], latent[:, cols],
                                                        start=(a == 0), stop=(a == 1))
                    last.then_inc(pe_aux, 1)
                else:
                    aux = aux_free(job)
                    for i in range(2):
                        tok = slice((2 * n + i) * P, (2 * n + i + 1) * P)
                        for a in range(2):
                            last = nc.tensor.matmul(aux[:, 256 * i:256 * i + 256], latent[:, tok], wv[:, a, :],
                                                    start=(a == 0), stop=(a == 1))
                    last.then_inc(pe_aux, 1)

            def run_aux(job):
                if job[0] == "maxima":
                    pe.wait_ge(mx_ready, job[1] + 1)
                    aux = aux_free(job)
                    nc.tensor.transpose(aux[0:GH * TPC, 0:P], mx_row[:, job[1] % 2, :], ident[:]).then_inc(pe_aux, 1)
                elif job[0] == "out":
                    pe.wait_ge(pv_done, job[1] + 1)
                    aux = aux_free(job)
                    for i in range(TPC):
                        last = nc.tensor.transpose(aux[:, P * i:P * i + P], out_t[:, P * i:P * i + P], ident[:])
                    last.then_inc(pe_aux, 1)
                else:
                    projection(job)

            def max_bank(bank):
                u, h, i, kb = bank
                c = u // UNITS_PER_CHUNK
                n = max_no[bank]
                pair = (u % UNITS_PER_CHUNK) * 2 + h // 2
                if n > MAX_BANKS:
                    pe.wait_ge(max_done, n - MAX_BANKS)
                last = kb == c
                cols = (i + 1) * P if last else CH
                ins = nc.tensor.matmul(max_ps[:, n % MAX_BANKS, 0:cols], q_stack[0:STACK, u % 4, h, i * P:(i + 1) * P],
                                       k_stack[0:STACK, pair, kb * CH:kb * CH + cols], start=True, stop=not last)
                if last:
                    ins = nc.tensor.matmul(max_ps[:, n % MAX_BANKS, i * P:(i + 1) * P], ident_b[:], mask_b[:],
                                           start=False, stop=True)
                ins.then_inc(pe_max, 1)

            def max_unit(u):
                c, g = divmod(u, UNITS_PER_CHUNK)
                pe.wait_ge(k_stacked, 16 * (2 * c + g // 2 + 1))
                pe.wait_ge(q_stacked, 16 * 2 * (u + 1))

            def score_head(s, h):
                u, b = steps[s]
                c, g = divmod(u, UNITS_PER_CHUNK)
                off = max(0, P * (b - TPC * c))
                n = GH * s + h
                if n >= SCORE_BANKS:
                    pe.wait_ge(exp_done, n - SCORE_BANKS + 1)
                elif n == SCORE_BANKS - 1:
                    wait_read(pe, prologue[len(prologue) // 2 * 2 - 1])
                if b == 0 and h == 0:
                    pe.wait_ge(m_stacked, 32 * (u + 1))
                    if c:
                        pe.wait_ge(ones_ready, c)
                nc.tensor.matmul(scores[:, n % SCORE_BANKS, off:CH], k_stack[:, 2 * g + h // 2, b * P:(b + 1) * P],
                                 q_stack[:, u % 4, h, off:CH], start=True, stop=True).then_inc(pe_scores, 1)

            def values(s):
                u, b = steps[s]
                c, g = divmod(u, UNITS_PER_CHUNK)
                off = max(0, P * (b - TPC * c))
                pe.wait_ge(exp_done, GH * (s + 1))
                if b >= TPC * c:
                    pe.wait_ge(mask_done, diag_before[s + 1])
                if b == 0:
                    if u:
                        pe.wait_ge(pv_done, u)
                    else:
                        pe.wait_ge(dve_consts, 2)
                    if g == 0:
                        wait_read(pe, ("value", c, 1))
                for h in range(GH):
                    last = nc.tensor.matmul(pv_ps[32 * h:32 * h + DH + 1, off:CH], v_ones[:, b, GH * g + h, :],
                                            probs[:, s % 2, h, off:CH],
                                            start=(b == 0), stop=(b == TPC * (c + 1) - 1),
                                            skip_group_check=True)
                last.then_inc(pe_pv, 1)

            def run_banks(banks):
                for bank in banks:
                    if bank[1:] == (0, 0, 0):
                        max_unit(bank[0])
                    max_bank(bank)

            def before_scores():
                for job in aux_at[-1]:
                    if job[0] == "maxima":
                        pe.wait_ge(consts_ready, 2)
                        run_banks(m for m in max_at[-1] if m[0] == job[1])
                    run_aux(job)
                run_banks(m for m in max_at[-1] if last_bank_at[m[0]] >= 0)

            before_scores()
            for s in range(END):
                banks, jobs = quarters(max_at[s]), quarters(aux_at[s], 2)
                for half in range(2):
                    for h in (2 * half, 2 * half + 1):
                        run_banks(banks[h])
                        if s < NS:
                            score_head(s, h)
                    for job in jobs[half]:
                        run_aux(job)
                    if half and 1 <= s <= NS:
                        values(s - 1)

        @block.vector
        def _(dve):
            chain = [0]

            def link(ins):
                chain[0] += 1
                ins.then_inc(dve_chain, 1)
                dve.wait_ge(dve_chain, chain[0])

            nc.vector.memset(pv_ps[:], 0.0).then_inc(dve_consts, 1)
            nc.vector.memset(v_ones[:, :, :, DH:DH + 1], 1.0).then_inc(dve_consts, 1)
            nc.vector.memset(q_stack[0:STACK, 2:4].bitcast(F32), 0.0).then_inc(zeros_high, 1)
            dve.wait_ge(hi_ready, 1)
            nc.vector.tensor_tensor(x_split[:, 1], x_raw[:], x_split[:, 0].bitcast(F32), ALU.subtract).then_inc(x_ready, 1)
            for n, (lo, hi) in enumerate(((OFF_D, OFF_K), (OFF_K, 2048), (OFF_Q, OFF_D))):
                dve.wait_ge(hi_ready, n + 2)
                nc.vector.tensor_tensor(w_split[:, 1, lo:hi], w_raw[:, lo:hi], w_split[:, 0, lo:hi].bitcast(F32),
                                        ALU.subtract).then_inc(w_ready, 1)

            def reduce_bank(bank):
                u, h, i, kb = bank
                c = u // UNITS_PER_CHUNK
                n = max_no[bank]
                cols = (i + 1) * P if kb == c else CH
                if u >= 2 and (h, i, kb) == (0, 0, 0):
                    dve.wait_ge(mx_ready, u - 1)
                dve.wait_ge(pe_max, n)
                nc.vector.tensor_reduce(mx[:, u % 2, h * TPC + i, kb:kb + 1], max_ps[:, n % MAX_BANKS, 0:cols], AX.X, ALU.max)\
                  .then_inc(max_done, 1)

            def fold_maxima(u):
                c = u // UNITS_PER_CHUNK
                dve.wait_ge(max_done, max_no[max_banks(u)[-1]])
                if u >= 2:
                    dve.wait_ge(pe_aux, aux_no[("maxima", u - 2)])
                nc.vector.tensor_reduce(mx_row[:, u % 2, :], mx[:, u % 2, :, 0:c + 1], AX.X, ALU.max)\
                  .then_inc(mx_ready, 1)

            def read_aux(job):
                dve.wait_ge(pe_aux, aux_no[job])
                kind = job[0]
                aux = aux_bank(job)
                if kind == "latent":
                    if job[1]:
                        dve.wait_ge(pe_aux, aux_no[("rope", job[1] - 1, 5)])
                        dve.wait_ge(dve_read, by_dve[("latent", job[1] - 1, 0)])
                    link(nc.vector.tensor_copy(latent_hi[LATENT:P], aux[LATENT:P]))
                    link(nc.vector.tensor_copy(latent[0:LATENT], aux[0:LATENT]))
                    nc.vector.tensor_tensor(latent[LATENT:P], aux[LATENT:P], latent_hi[LATENT:P].bitcast(F32),
                                            ALU.subtract).then_inc(dve_read, 1)
                elif kind == "maxima":
                    u = job[1]
                    src = aux[0:GH * TPC, 0:P]
                    if u >= 2:
                        dve.wait_ge(m_stacked, 32 * (u - 1))
                    link(nc.vector.tensor_scalar(m_rows[:, u % 2, 0, :], src, -1.0, None, ALU.mult))
                    nc.vector.scalar_tensor_tensor(out=m_rows[:, u % 2, 1, :], in0=src, scalar=-1.0,
                                                   in1=m_rows[:, u % 2, 0, :].bitcast(F32), op0=ALU.mult,
                                                   op1=ALU.subtract).then_inc(dve_read, 1)
                else:
                    normalise(job)

            def normalise(job):
                u = job[1]
                c, g = divmod(u, UNITS_PER_CHUNK)
                v = aux_bank(job).rearrange("p (i h d) -> p i h d", i=TPC, h=GH)
                if u:
                    dve.wait_ge(dve_read, by_dve[("out", u - 1)])
                link(nc.vector.reciprocal(recip[:], v[:, :, :, DH]))
                a = attn[:, :, g * GH * DH:(g + 1) * GH * DH].rearrange("p i (h d) -> p i h d", h=GH)
                nc.vector.tensor_tensor(a, v[:, :, :, 0:DH],
                                        recip[:].unsqueeze(3).to_broadcast([P, TPC, GH, DH]), ALU.mult)\
                  .then_inc(dve_read, 1)

            def variance(c):
                dve.wait_ge(dve_read, by_dve[("out", c * UNITS_PER_CHUNK + UNITS_PER_CHUNK - 1)])
                dve.wait_ge(tok_loaded, 16 * (c + 1))
                if c:
                    dve.wait_ge(x1_stored, 16 * c)
                    dve.wait_ge(x1_ready, c)
                link(nc.vector.tensor_tensor(summed[:], attn[:], x_tok[:], ALU.add))
                for i in range(TPC):
                    last = nc.vector.bn_stats(stats[:, i, :], summed[:, i, :])
                link(last)
                for i in range(TPC):
                    last = nc.vector.bn_aggr(mean_var[:, i, :], stats[:, i, :])
                link(last)
                nc.vector.tensor_scalar(var_eps[:], mean_var[:, :, 1], EPS, None, ALU.add).then_inc(var_ready, 1)

            def layer_norm(c):
                dve.wait_ge(rstd_ready, c + 1)
                for i in range(TPC):
                    last = nc.vector.tensor_scalar(summed[:, i, :], summed[:, i, :], mean_var[:, i, 0:1],
                                                   rstd[:, i:i + 1], ALU.subtract, ALU.mult)
                last.then_inc(x1_ready, 1)

            for job in aux_at[-1]:
                if job[0] == "maxima":
                    for bank in max_at[-1]:
                        if bank[0] == job[1]:
                            reduce_bank(bank)
                    fold_maxima(job[1])
                if job in by_dve:
                    read_aux(job)
                elif job[0] == "rope" and job[1] == 0:
                    rotate(dve, nc.vector, job, link)
            for bank in max_at[-1]:
                if last_bank_at[bank[0]] >= 0:
                    reduce_bank(bank)
            for s in range(END):
                banks, jobs = quarters(max_at[s]), quarters(aux_at[s], 2)
                for k in range(4):
                    for bank in banks[k]:
                        reduce_bank(bank)
                    if k == 0 and s:
                        for job in aux_at[s - 1]:
                            if job[0] == "rope" and job[1] == 0:
                                rotate(dve, nc.vector, job, link)
                    if k % 2:
                        for job in jobs[k // 2]:
                            if job in by_dve:
                                read_aux(job)
                for u in range(UNITS):
                    if last_bank_at[u] == s:
                        fold_maxima(u)
                if s in norm_at:
                    variance(norm_at[s])
                if s - 1 in norm_at:
                    layer_norm(norm_at[s - 1])


INTER = 176
EXPERTS = 16
TOP_K = 2
HALF = INTER // 2
RANKS_AT = 8
RING = 4


def build_experts(nc, t, x1_dram, out):
    S, E = out.shape
    TT = S // P
    KT = E // P
    SLOTS = (S * TOP_K + EXPERTS * (P - 1)) // P
    SHARED = 2 * TT
    ITEMS = SHARED + SLOTS

    TOKEN, BEST, WEIGHTS, ROW = E, E + 1, E + 2, E + 4
    slot_x = nc.dram_tensor("slot_x", (SLOTS * P, ROW), F32, kind="Internal").ap()
    token_y = nc.dram_tensor("token_y", (TOP_K * S + RING * P, E), F32, kind="Internal").ap()

    with ExitStack() as ctx:
        def sb(name, shape, dt=F32):
            return ctx.enter_context(nc.sbuf_tensor(name, shape, dt))

        def ps(name, shape):
            return ctx.enter_context(nc.psum_tensor(name, shape, F32))

        def sem(name):
            return ctx.enter_context(nc.semaphore(name))

        w_up = sb("w_up_sb", [P, EXPERTS + 2, KT, 2 * INTER])
        w_dn = sb("w_dn_sb", [HALF, EXPERTS + 2, 2, E])
        x1 = sb("x1_sb", [P, TT, ROW])
        x1_t = sb("x1_t", [P, KT, S])
        base = sb("base", [P, TT, E])
        gate = sb("gate_sb", [P, KT, EXPERTS])
        consts = sb("consts_sb", [P, 16 + 16 + 256 + 48 + TT + RING])
        ident = sb("ident2", [P, P])
        before_b = sb("before_b", [P, P], BF16)
        ones_b = sb("ones_b", [P, P], BF16)
        blank = sb("blank", [P, RING, ROW])
        power = sb("power2", [P, TPC])
        shifted = sb("shifted", [P, TT, EXPERTS])
        probs = sb("probs2", [P, TT, EXPERTS])
        row = sb("row", [P, 4, TT])
        best = sb("best", [P, TT, 8])
        best_at = sb("best_at", [P, TT, 8], U32)
        best_f = sb("best_f", [P, 2, TT])
        chosen = sb("chosen", [P, 2, TT, EXPERTS])
        member = sb("member", [P, TT + 1, EXPERTS], BF16)
        count = sb("count", [P, EXPERTS])
        grid = sb("grid", [P, EXPERTS, TT])
        tiles = sb("tiles", [P, 3, EXPERTS])
        grid2 = sb("grid2", [P, 48, EXPERTS])
        expert_f = sb("expert_f", [P, 48])
        expert = sb("expert", [P, 48], I32)
        place = sb("place", [P, TT, EXPERTS])
        place_of = sb("place_of", [P, TT, EXPERTS])
        slot_f = sb("slot_f", [P, 2, TT])
        slot = sb("slot", [P, 2, TT], I32)
        xg = sb("xg", [P, RING, ROW])
        xg_t = sb("xg_t", [P, 2, KT, P])
        silu = sb("silu", [P, 2, INTER])
        hidden = sb("hidden", [P, 2, INTER])
        hidden_t = sb("hidden_t", [HALF, 2, 2, P])
        part_w = sb("part_w", [P, RING, 2])
        weight = sb("weight", [P, RING])
        second = sb("second", [P, RING])
        dest = sb("dest", [P, RING], I32)
        ys = sb("ys", [P, RING, E])
        yg = sb("yg", [P, 2, TOP_K, TPC, E])
        stats = sb("stats2", [P, TT, 6])
        mean_var = sb("mean_var2", [P, TT, 2])
        var_eps = sb("var_eps2", [P, TT])
        rstd = sb("rstd2", [P, TT])
        neg_mean = sb("neg_mean", [P, TT])
        shift = sb("shift", [P, TT])

        xt_ps = ps("xt_ps", [P, 2, 512])
        gu_ps = ps("gu_ps", [P, 2, 512])
        ht_ps = ps("ht_ps", [P, 2, 512])
        y_ps = ps("y_ps", [P, 2, 512])

        small_loaded = sem("small_loaded")
        x1_loaded = [sem(f"x1_loaded{b}") for b in range(TT // TPC)]
        shared_loaded = sem("shared_loaded")
        experts_loaded = sem("experts_loaded")
        zeros_ready = sem("zeros_ready")
        slots_cleared = sem("slots_cleared")
        consts2_ready = sem("consts2_ready")
        pe_x1t = sem("pe_x1t")
        x1t_copied = sem("x1t_copied")
        x1t_even = sem("x1t_even")
        pe_logits = sem("pe_logits")
        shift_ready = sem("shift_ready")
        exps_ready = sem("exps_ready")
        members_ready = sem("members_ready")
        pe_ranks = sem("pe_ranks")
        slots_ready = sem("slots_ready")
        experts_ready = sem("experts_ready")
        scattered = sem("scattered")
        chain_sem = sem("dve_chain2")
        xg_loaded = [sem(f"xg_loaded{r}") for r in range(RING)]
        ys_stored = [sem(f"ys_stored{r}") for r in range(RING)]
        pe_xt = sem("pe_xt")
        xt_copied = sem("xt_copied")
        pe_gu = sem("pe_gu")
        silu_done = sem("silu_done")
        hidden_done = sem("hidden_done")
        pe_ht = sem("pe_ht")
        ht_copied = sem("ht_copied")
        pe_y = sem("pe_y")
        y_taken = sem("y_taken")
        results_loaded = [[sem(f"results_loaded{r}_{k}") for k in range(TOP_K)] for r in range(2)]
        route_step = sem("route_step")
        routed = sem("routed")
        store_begun = sem("store_begun")
        shift2_ready = sem("shift2_ready")
        sums_ready = sem("sums_ready")
        var2_ready = sem("var2_ready")
        rstd2_ready = sem("rstd2_ready")
        rows_ready = sem("rows_ready")
        rows_stored = sem("rows_stored")

        iota_e = consts[:, 0:16]
        step_128 = consts[:, 16:32]
        earlier = consts[:, 32:288].rearrange("p (e f) -> p e f", e=EXPERTS)
        iota_slot = consts[:, 288:336]
        token_no = consts[:, 336:336 + TT]
        spare_row = consts[:, 336 + TT:]

        def loads_of(j, j0):
            return (j - j0) * (16 // RING) + 16 * (j0 // RING + 1)

        LEAD = RING + 2
        TURNS = (SLOTS - 1 - LEAD) // RING
        LOOP_END = LEAD + RING * TURNS

        block = ctx.enter_context(nc.Block())

        def over_slots(eng, body, end):
            for j in range(LEAD):
                body(j, j % RING, j)
            with eng.Fori(0, TURNS) as turn:
                for k in range(RING):
                    body(turn * RING + (LEAD + k), (LEAD + k) % RING, LEAD + k)
            for j in range(LOOP_END, end):
                body(j, j % RING, j)

        def load_results(eng, k):
            for r in range(RING):
                eng.wait_ge(ys_stored[r], 16 * ((SLOTS - 1 - r) // RING + 1))
            for b in range(TT // TPC):
                if b >= 2:
                    eng.wait_ge(sums_ready, 2 * (b - 1))
                    eng.wait_ge(results_loaded[b % 2][k], 16 * (b // 2))
                eng.dma_start(yg[:, b % 2, k], token_y[k * S + b * CH:k * S + (b + 1) * CH]
                              .rearrange("(i p) n -> p i n", p=P)).then_inc(results_loaded[b % 2][k], 16)

        @block.sync
        def _(sp):
            for b in range(TT // TPC):
                sp.dma_start(x1[:, b * TPC:(b + 1) * TPC, 0:E],
                             x1_dram[b * CH:(b + 1) * CH].rearrange("(i p) n -> p i n", p=P)).then_inc(x1_loaded[b], 16)
            sp.dma_start(gate[:], t["gate"]).then_inc(small_loaded, 16)
            sp.dma_start(consts[:], t["consts"]).then_inc(small_loaded, 16)
            sp.dma_start(w_up[:, EXPERTS:], t["w_up"][:, EXPERTS:]).then_inc(shared_loaded, 16)
            sp.dma_start(w_dn[:, EXPERTS:], t["w_dn"][:, EXPERTS:]).then_inc(shared_loaded, 16)
            sp.wait_ge(zeros_ready, 3)
            for j in range(0, SLOTS, RING):
                n = min(RING, SLOTS - j)
                sp.dma_start(slot_x[j * P:(j + n) * P].rearrange("(i p) n -> p i n", p=P),
                             blank[:, 0:n]).then_inc(slots_cleared, 16)
            for e in range(0, EXPERTS, 4):
                sp.dma_start(w_up[:, e:e + 4], t["w_up"][:, e:e + 4]).then_inc(experts_loaded, 16)
                sp.dma_start(w_dn[:, e:e + 4], t["w_dn"][:, e:e + 4]).then_inc(experts_loaded, 16)
            sp.wait_ge(scattered, 16 * TOP_K * TT)

            def load(j, r, j0):
                if j0 >= RING:
                    sp.wait_ge(pe_xt, j + (1 - RING))
                    sp.wait_ge(routed, 2 * j + 2 * (1 - RING))
                sp.dma_start(xg[:, r, :], slot_x[bass.ds(j * P, P), :]).then_inc(xg_loaded[r], 16)

            over_slots(sp, load, SLOTS)
            load_results(sp, 0)
            for b in range(TT // TPC):
                sp.wait_ge(rows_ready, b + 1)
                sp.dma_start(out[b * CH:(b + 1) * CH].rearrange("(i p) n -> p i n", p=P),
                             base[:, b * TPC:(b + 1) * TPC]).then_inc(rows_stored, 16)
            sp.wait_ge(rows_stored, 16 * (TT // TPC))

        @block.gpsimd
        def _(pool):
            nc.gpsimd.memset(ident[:], 0.0).then_inc(consts2_ready, 1)
            nc.gpsimd.memset(ones_b[:], 1.0).then_inc(consts2_ready, 1)
            nc.gpsimd.memset(power[:], -0.5).then_inc(consts2_ready, 1)
            nc.gpsimd.memset(member[:, TT, :], 0.0).then_inc(consts2_ready, 1)
            nc.gpsimd.memset(blank[:], 0.0).then_inc(zeros_ready, 1)
            pool.wait_ge(zeros_ready, 1)
            nc.gpsimd.memset(blank[:, :, BEST:BEST + 1], -1.0).then_inc(zeros_ready, 1)
            pool.wait_ge(consts2_ready, 4)
            nc.gpsimd.affine_select(out=ident[:], in_=ident[:], compare_op=ALU.not_equal, fill=1.0, base=0,
                                    pattern=[[-1, P]], channel_multiplier=1).then_inc(consts2_ready, 1)
            nc.gpsimd.affine_select(out=before_b[:], in_=ones_b[:], compare_op=ALU.is_gt, fill=0.0, base=0,
                                    pattern=[[1, P]], channel_multiplier=-1).then_inc(consts2_ready, 1)
            pool.wait_ge(small_loaded, 32)
            nc.gpsimd.tensor_copy(blank[:, :, TOKEN], spare_row).then_inc(zeros_ready, 1)
            pool.wait_ge(slots_ready, 1)
            pool.wait_ge(slots_cleared, 16 * ((SLOTS + RING - 1) // RING))
            for b in range(TT // TPC):
                pool.wait_ge(x1_loaded[b], 16)
            for i in range(TT):
                for k in range(TOP_K):
                    pool.indirect_dma_start(out=slot_x, out_offset=bass.IndirectOffsetOnAxis(ap=slot[:, k, i:i + 1], axis=0),
                                            in_=x1[:, i, :], in_offset=None).then_inc(scattered, 16)

            def store(j, r, j0):
                pool.wait_ge(y_taken, j + (TT + 1))
                pool.wait_ge(routed, 2 * j + 2)
                pool.sem_inc(store_begun)
                pool.indirect_dma_start(out=token_y, out_offset=bass.IndirectOffsetOnAxis(ap=dest[:, r:r + 1], axis=0),
                                        in_=ys[:, r, :], in_offset=None).then_inc(ys_stored[r], 16)

            over_slots(pool, store, SLOTS)
            for b in range(TT // TPC):
                at = slice(b * TPC, (b + 1) * TPC)
                pool.wait_ge(var2_ready, 2 * (b + 1))
                nc.gpsimd.tensor_tensor(rstd[:, at], var_eps[:, at], power[:], ALU.pow).then_inc(rstd2_ready, 1)
                pool.wait_ge(rstd2_ready, b + 1)
                nc.gpsimd.tensor_tensor(shift[:, at], neg_mean[:, at], rstd[:, at], ALU.mult).then_inc(shift2_ready, 1)

        @block.scalar
        def _(act):
            for p in range(1, TT // 2, 2):
                act.wait_ge(pe_x1t, p + 1)
                nc.scalar.activation(x1_t[:, :, 2 * p * P:2 * (p + 1) * P].rearrange("p k (i n) -> p k i n", i=2),
                                     xt_ps[:, p % 2].rearrange("p (i k n) -> p k i n", i=2, k=KT), ACT.Copy)\
                  .then_inc(x1t_copied, 1)
            act.wait_ge(shift_ready, 1)
            nc.scalar.activation(probs[:], shifted[:], ACT.Exp).then_inc(exps_ready, 1)

            def gate_of(n, par, n0):
                act.wait_ge(pe_gu, n + 1)
                if n0 >= 2:
                    act.wait_ge(hidden_done, n - 1)
                nc.scalar.activation(silu[:, par], gu_ps[:, par, 0:INTER], ACT.Silu).then_inc(silu_done, 1)

            for n in range(SHARED):
                gate_of(n, n % 2, n)

            def slot_tile(j, r, j0):
                act.wait_ge(pe_xt, j + 1)
                if j0 >= 2:
                    act.wait_ge(pe_gu, j + (SHARED - 1))
                nc.scalar.activation(xg_t[:, j0 % 2], xt_ps[:, j0 % 2, 0:E].rearrange("p (k n) -> p k n", k=KT), ACT.Copy)\
                  .then_inc(xt_copied, 1)
                if j0:
                    gate_of(j + (SHARED - 1), (j0 + 1) % 2, SHARED)

            over_slots(act, slot_tile, SLOTS)
            gate_of(ITEMS - 1, (ITEMS - 1) % 2, SHARED)
            load_results(act, 1)
            for b in range(TT // TPC):
                act.wait_ge(shift2_ready, b + 1)
                for i in range(b * TPC, (b + 1) * TPC):
                    last = nc.scalar.activation(base[:, i, :], base[:, i, :], ACT.Identity, bias=shift[:, i:i + 1],
                                                scale=rstd[:, i:i + 1])
                last.then_inc(rows_ready, 1)

        @block.tensor
        def _(pe):
            pe.wait_ge(consts2_ready, 6)
            for p in range(TT // 2):
                if p % 2 == 0:
                    pe.wait_ge(x1_loaded[p // 2], 16)
                if p >= 2:
                    pe.wait_ge(x1t_even if p % 2 == 0 else x1t_copied, p // 2)
                for i in range(2):
                    for k in range(KT):
                        last = nc.tensor.transpose(xt_ps[:, p % 2, (2 * i + k) * P:(2 * i + k + 1) * P],
                                                   x1[:, 2 * p + i, k * P:(k + 1) * P], ident[:])
                last.then_inc(pe_x1t, 1)
            pe.wait_ge(x1t_even, TT // 4)
            pe.wait_ge(x1t_copied, TT // 4)
            pe.wait_ge(small_loaded, 32)
            for i in range(TT):
                for k in range(KT):
                    last = nc.tensor.matmul(xt_ps[:, 0, i * EXPERTS:(i + 1) * EXPERTS], x1_t[:, k, i * P:(i + 1) * P],
                                            gate[:, k, :], start=(k == 0), stop=(k == KT - 1))
            last.then_inc(pe_logits, 1)

            def ranks():
                pe.wait_ge(members_ready, 1)
                r = xt_ps[:, 1, 0:(TT + 1) * EXPERTS].rearrange("p (i e) -> p i e", e=EXPERTS)
                nc.tensor.matmul(r, before_b[:], member[:], start=True, stop=False)
                for i in range(TT):
                    last = nc.tensor.matmul(r[:, i + 1:, :], ones_b[:],
                                            member[:, i:i + 1, :].to_broadcast([P, TT - i, EXPERTS]),
                                            start=False, stop=(i == TT - 1))
                last.then_inc(pe_ranks, 1)

            def up(n, par, n0, x_of, e):
                if n0 >= 2:
                    pe.wait_ge(hidden_done, n - 1)
                for k in range(KT):
                    last = nc.tensor.matmul(gu_ps[:, par, 0:2 * INTER], x_of(k), w_up[:, e, k, :],
                                            start=(k == 0), stop=(k == KT - 1))
                last.then_inc(pe_gu, 1)

            def turn_hidden(n, par, n0):
                pe.wait_ge(hidden_done, n + 1)
                if n0 >= 2:
                    pe.wait_ge(ht_copied, n - 1)
                for k in range(2):
                    last = nc.tensor.transpose(ht_ps[0:HALF, par, k * P:(k + 1) * P],
                                               hidden[:, par, k * HALF:(k + 1) * HALF], ident[:])
                last.then_inc(pe_ht, 1)

            def down(n, par, bank, group, e, start=True, stop=True):
                pe.wait_ge(ht_copied, n + 1)
                if start and group is not None:
                    pe.wait_ge(y_taken, group)
                for k in range(2):
                    last = nc.tensor.matmul(y_ps[:, bank, 0:E], hidden_t[:, par, k, :], w_dn[:, e, k, :],
                                            start=(start and k == 0), stop=(stop and k == 1))
                last.then_inc(pe_y, 1)

            def down_shared(n):
                i, half = divmod(n, 2)
                down(n, n % 2, i % 2, i - 1 if i >= 2 else None, EXPERTS + half, half == 0, half == 1)

            pe.wait_ge(shared_loaded, 32)
            for n in range(SHARED):
                i, half = divmod(n, 2)
                up(n, n % 2, n, lambda k: x1_t[:, k, i * P:(i + 1) * P], EXPERTS + half)
                if n >= 1:
                    turn_hidden(n - 1, (n - 1) % 2, n - 1)
                if n >= 2:
                    down_shared(n - 2)
                if n == RANKS_AT:
                    ranks()

            def turn_rows(j, r, par, j0):
                pe.wait_ge(xg_loaded[r], loads_of(j, j0))
                if j0 >= 2:
                    pe.wait_ge(xt_copied, j - 1)
                for k in range(KT):
                    last = nc.tensor.transpose(xt_ps[:, par, k * P:(k + 1) * P], xg[:, r, k * P:(k + 1) * P], ident[:])
                last.then_inc(pe_xt, 1)

            def expert_of(j):
                return pe.value_load(expert[0:1, bass.ds(j, 1)], min_val=0, max_val=EXPERTS - 1)

            def slot_tile(j, r, j0):
                if j0 == 0:
                    pe.wait_ge(experts_ready, 1)
                    pe.wait_ge(experts_loaded, 16 * 2 * 4)
                    pe.wait_ge(slots_ready, 1)
                    turn_rows(0, 0, 0, 0)
                if j0 + 1 < SLOTS:
                    turn_rows(j + 1, (r + 1) % RING, (j0 + 1) % 2, j0 + 1)
                pe.wait_ge(xt_copied, j + 1)
                up(j + SHARED, j0 % 2, SHARED, lambda k: xg_t[:, j0 % 2, k, :], bass.ds(expert_of(j), 1))
                turn_hidden(j + (SHARED - 1), (j0 + 1) % 2, SHARED)
                if j0 < 2:
                    down_shared(SHARED - 2 + j0)
                else:
                    down(j + (SHARED - 2), j0 % 2, (TT + j0) % 2, j + (TT - 3), bass.ds(expert_of(j - 2), 1))

            over_slots(pe, slot_tile, SLOTS)
            turn_hidden(ITEMS - 1, (ITEMS - 1) % 2, SHARED)
            for j in range(SLOTS - 2, SLOTS):
                down(j + SHARED, j % 2, (TT + j) % 2, j + TT - 1, bass.ds(expert_of(j), 1))

        @block.vector
        def _(dve):
            chain = [0]

            def link(ins):
                chain[0] += 1
                ins.then_inc(chain_sem, 1)
                dve.wait_ge(chain_sem, chain[0])

            for p in range(0, TT // 2, 2):
                dve.wait_ge(pe_x1t, p + 1)
                nc.vector.tensor_copy(x1_t[:, :, 2 * p * P:2 * (p + 1) * P].rearrange("p k (i n) -> p k i n", i=2),
                                      xt_ps[:, p % 2].rearrange("p (i k n) -> p k i n", i=2, k=KT))\
                  .then_inc(x1t_even, 1)

            def along_e(v):
                return v.unsqueeze(2).to_broadcast([P, TT, EXPERTS])

            def softmax():
                dve.wait_ge(pe_logits, 1)
                dve.wait_ge(small_loaded, 32)
                logits = xt_ps[:, 0, 0:TT * EXPERTS].rearrange("p (i e) -> p i e", e=EXPERTS)
                link(nc.vector.tensor_reduce(row[:, 0, :], logits, AX.X, ALU.max))
                nc.vector.tensor_tensor(shifted[:], logits, along_e(row[:, 0, :]), ALU.subtract).then_inc(shift_ready, 1)

            def scale_probs():
                dve.wait_ge(exps_ready, 1)
                link(nc.vector.tensor_reduce(row[:, 1, :], probs[:], AX.X, ALU.add))
                link(nc.vector.reciprocal(row[:, 2, :], row[:, 1, :]))
                link(nc.vector.tensor_tensor(shifted[:], probs[:], along_e(row[:, 2, :]), ALU.mult))

            def top_two(tiles_of):
                for i in tiles_of:
                    link(nc.vector.max(best[:, i, :], shifted[:, i, :]))
                    last = nc.vector.max_index(best_at[:, i, :], best[:, i, :], shifted[:, i, :])
                link(last)

            def memberships():
                link(nc.vector.tensor_copy(best_f[:].rearrange("p k i -> p i k"), best_at[:, :, 0:TOP_K]))
                for k in range(TOP_K):
                    link(nc.vector.tensor_tensor(chosen[:, k], iota_e.unsqueeze(1).to_broadcast([P, TT, EXPERTS]),
                                                 along_e(best_f[:, k, :]), ALU.is_equal))
                dve.wait_ge(consts2_ready, 6)
                nc.vector.tensor_tensor(member[:, 0:TT, :], chosen[:, 0], chosen[:, 1], ALU.add).then_inc(members_ready, 1)

            def slots_of():
                dve.wait_ge(pe_ranks, 1)
                r = xt_ps[:, 1, 0:(TT + 1) * EXPERTS].rearrange("p (i e) -> p i e", e=EXPERTS)
                link(nc.vector.tensor_copy(count[:], r[:, TT, :]))
                link(nc.vector.tensor_tensor(grid[:], count[:].unsqueeze(2).to_broadcast([P, EXPERTS, TT]),
                                             step_128.unsqueeze(1).to_broadcast([P, EXPERTS, TT]), ALU.is_gt))
                link(nc.vector.tensor_reduce(tiles[:, 0, :], grid[:], AX.X, ALU.add))
                link(nc.vector.tensor_tensor(grid[:], tiles[:, 0:1, :].to_broadcast([P, EXPERTS, EXPERTS]), earlier, ALU.mult))
                link(nc.vector.tensor_reduce(tiles[:, 1, :], grid[:], AX.X, ALU.add))
                link(nc.vector.tensor_scalar(count[:], tiles[:, 1, :], float(P), None, ALU.mult))
                link(nc.vector.tensor_tensor(place[:], r[:, 0:TT, :], count[:].unsqueeze(1).to_broadcast([P, TT, EXPERTS]), ALU.add))
                for k in range(TOP_K):
                    link(nc.vector.tensor_tensor(place_of[:], place[:], chosen[:, k], ALU.mult))
                    link(nc.vector.tensor_reduce(slot_f[:, k, :], place_of[:], AX.X, ALU.add))
                link(nc.vector.tensor_copy(x1[:, :, TOKEN], token_no))
                link(nc.vector.tensor_copy(x1[:, :, BEST], best_f[:, 0, :]))
                link(nc.vector.tensor_copy(x1[:, :, WEIGHTS:ROW], best[:, :, 0:TOP_K]))
                nc.vector.tensor_copy(slot[:], slot_f[:]).then_inc(slots_ready, 1)

            def experts_of():
                link(nc.vector.tensor_tensor(tiles[:, 2, :], tiles[:, 0, :], tiles[:, 1, :], ALU.add))
                link(nc.vector.tensor_tensor(grid2[:], tiles[:, 2:3, :].to_broadcast([P, 48, EXPERTS]),
                                             iota_slot.unsqueeze(2).to_broadcast([P, 48, EXPERTS]), ALU.is_le))
                link(nc.vector.tensor_reduce(expert_f[:], grid2[:], AX.X, ALU.add))
                nc.vector.tensor_scalar(expert[:], expert_f[:], float(EXPERTS - 1), None, ALU.min).then_inc(experts_ready, 1)

            def hide(n, par, n0):
                dve.wait_ge(silu_done, n + 1)
                if n0 >= 2:
                    dve.wait_ge(pe_ht, n - 1)
                nc.vector.tensor_tensor(hidden[:, par], silu[:, par], gu_ps[:, par, INTER:2 * INTER], ALU.mult)\
                  .then_inc(hidden_done, 1)

            def copy_hidden(n, par, n0):
                dve.wait_ge(pe_ht, n + 1)
                if n0 >= 2:
                    dve.wait_ge(pe_y, n - 1)
                nc.vector.tensor_copy(hidden_t[:, par], ht_ps[0:HALF, par, 0:2 * P].rearrange("p (k n) -> p k n", k=2))\
                  .then_inc(ht_copied, 1)

            def take_shared(i):
                dve.wait_ge(pe_y, 2 * i + 2)
                nc.vector.tensor_tensor(base[:, i, :], x1[:, i, 0:E], y_ps[:, i % 2, 0:E], ALU.add).then_inc(y_taken, 1)

            stages = {0: softmax, 1: scale_probs, 2: lambda: top_two(range(0, 4)), 3: lambda: top_two(range(4, 8)),
                      4: lambda: top_two(range(8, 12)), 5: lambda: top_two(range(12, 16)), 6: memberships,
                      RANKS_AT + 1: slots_of, RANKS_AT + 2: experts_of}
            for b in range(TT // TPC):
                dve.wait_ge(x1_loaded[b], 16)
            softmax()
            for n in range(SHARED):
                if n in stages and n:
                    stages[n]()
                hide(n, n % 2, n)
                if n >= 1:
                    copy_hidden(n - 1, (n - 1) % 2, n - 1)
                if n >= 3 and n % 2:
                    take_shared((n - 3) // 2)

            def route(j, r, j0):
                if j0 >= RING:
                    dve.wait_ge(ys_stored[r], loads_of(j, j0) - 16)
                dve.wait_ge(xg_loaded[r], loads_of(j, j0))
                own, best_of = expert_f[:, bass.ds(j, 1)], xg[:, r, BEST:BEST + 1]
                for k, op in enumerate((ALU.is_equal, ALU.not_equal)):
                    nc.vector.scalar_tensor_tensor(out=part_w[:, r, k:k + 1], in0=best_of, scalar=own,
                                                   in1=xg[:, r, WEIGHTS + k:WEIGHTS + k + 1], op0=op, op1=ALU.mult)\
                      .then_inc(route_step, 1)
                nc.vector.tensor_scalar(second[:, r:r + 1], best_of, own, float(S), ALU.not_equal, ALU.mult)\
                  .then_inc(route_step, 1)
                dve.wait_ge(route_step, 3 * j + 3)
                nc.vector.tensor_tensor(weight[:, r:r + 1], part_w[:, r, 0:1], part_w[:, r, 1:2], ALU.add).then_inc(routed, 1)
                nc.vector.tensor_tensor(dest[:, r:r + 1], second[:, r:r + 1], xg[:, r, TOKEN:TOKEN + 1], ALU.add)\
                  .then_inc(routed, 1)

            def take(j, r, j0):
                dve.wait_ge(pe_y, j + (SHARED + 1))
                dve.wait_ge(routed, 2 * j + 2)
                nc.vector.tensor_scalar(ys[:, r, :], y_ps[:, (TT + j0) % 2, 0:E], weight[:, r:r + 1], None, ALU.mult)\
                  .then_inc(y_taken, 1)

            def slot_tile(j, r, j0):
                route(j, r, j0)
                hide(j + SHARED, j0 % 2, SHARED)
                copy_hidden(j + (SHARED - 1), (j0 + 1) % 2, SHARED)
                if j0 < 2:
                    if j0 == 1:
                        take_shared(TT - 1)
                else:
                    take(j - 2, (r + 2) % RING, j0 - 2)

            over_slots(dve, slot_tile, SLOTS)
            copy_hidden(ITEMS - 1, (ITEMS - 1) % 2, SHARED)
            for j in range(SLOTS - 2, SLOTS):
                take(j, j % RING, j)

            for b in range(TT // TPC):
                at = slice(b * TPC, (b + 1) * TPC)
                for k in range(TOP_K):
                    dve.wait_ge(results_loaded[b % 2][k], 16 * (b // 2 + 1))
                    nc.vector.tensor_tensor(base[:, at, :], base[:, at, :], yg[:, b % 2, k], ALU.add).then_inc(sums_ready, 1)
                    dve.wait_ge(sums_ready, 2 * b + k + 1)
                for i in range(b * TPC, (b + 1) * TPC):
                    last = nc.vector.bn_stats(stats[:, i, :], base[:, i, :])
                link(last)
                for i in range(b * TPC, (b + 1) * TPC):
                    last = nc.vector.bn_aggr(mean_var[:, i, :], stats[:, i, :])
                link(last)
                nc.vector.tensor_scalar(var_eps[:, at], mean_var[:, at, 1], EPS, None, ALU.add).then_inc(var2_ready, 1)
                nc.vector.tensor_scalar(neg_mean[:, at], mean_var[:, at, 0], -1.0, None, ALU.mult).then_inc(var2_ready, 1)


def build_program(nc, t, out):
    x1_dram = nc.dram_tensor("x1_rows", out.shape, F32, kind="Internal").ap()
    build_attention(nc, t, x1_dram)
    build_experts(nc, t, x1_dram, out)


def layout(inputs):
    a = {k.removeprefix("L0_"): np.asarray(v) for k, v in inputs.items()}
    x = a["attn_x"][0]
    S = x.shape[0]
    even, odd = list(range(NOPE, DH, 2)), list(range(NOPE + 1, DH, 2))
    own = list(range(NOPE)) + even + odd
    partner = list(range(NOPE)) + odd + even
    cols = [(m + 2 * j + two) * DH + d for order in (own, partner) for m in (0, 8) for two in range(2)
            for d in order for j in range(GH)]
    freqs = np.float32(1.0) / np.float32(THETA) ** (np.arange(0, ROPE_D, 2, dtype=np.float32) / np.float32(ROPE_D))
    angle = np.arange(S, dtype=np.float32)[:, None] * freqs[None, :]
    cos, sin = np.cos(angle).T, np.sin(angle).T
    head = np.zeros((2, DH, S), np.float32)
    head[0, :NOPE] = 1.0
    head[0, NOPE:] = np.concatenate([cos, cos])
    head[1, NOPE:] = np.concatenate([-sin, sin])
    w1, w2, w3 = (a[f"ffn_w{n}"] for n in (1, 2, 3))
    s1, s3 = (a[f"ffn_sw{n}"].reshape(2, INTER, -1) for n in (1, 3))
    s2 = a["ffn_sw2"].reshape(-1, 2, INTER).transpose(1, 0, 2)
    up = np.concatenate([np.concatenate([w1, s1]), np.concatenate([w3, s3])], axis=1).transpose(0, 2, 1)
    down = np.concatenate([w2, s2]).transpose(0, 2, 1)
    n16 = np.arange(EXPERTS, dtype=np.float32)
    consts = np.concatenate([n16, n16 * P, (n16[None, :] < n16[:, None]).astype(np.float32).ravel(),
                             np.arange(48, dtype=np.float32)])
    token = np.arange(S, dtype=np.float32).reshape(-1, P).T
    spare = S + np.arange(RING * P, dtype=np.float32).reshape(-1, P).T
    consts = np.ascontiguousarray(np.concatenate([np.broadcast_to(consts, (P, consts.size)), token, spare], axis=1))
    c = np.ascontiguousarray
    return {
        "x": c(x), "xT": c(x.T),
        "w_q": c(a["attn_Wq"][:, cols]),
        "w_down": c(np.concatenate([a["attn_Wkv_down"]] * 2, axis=1)),
        "w_k": c(np.concatenate([a["attn_Wk_up"][:, cols]] * 2, axis=0)),
        "w_v": c(np.concatenate([a["attn_Wv_up"]] * 2, axis=0)),
        "gate": c(a["ffn_gate_w"].T.reshape(2, P, EXPERTS).transpose(1, 0, 2)),
        "w_up": c(up.reshape(EXPERTS + 2, 2, P, 2 * INTER).transpose(2, 0, 1, 3)),
        "w_dn": c(down.reshape(EXPERTS + 2, 2, HALF, 256).transpose(2, 0, 1, 3)),
        "consts": consts,
        "rope": c(np.concatenate([np.repeat(head, GH, axis=1)] * 2, axis=1).transpose(1, 0, 2)),
    }


def kernel(**inputs):
    from concourse import bacc
    from concourse.bass_utils import run_bass_kernel_spmd

    arrays = layout(inputs)
    S, E = arrays["x"].shape
    nc = bacc.Bacc("TRN2", target_bir_lowering=False, num_devices=1)
    t = {name: nc.dram_tensor(name, a.shape, mybir.dt.from_np(a.dtype), kind="ExternalInput").ap()
         for name, a in arrays.items()}
    out = nc.dram_tensor("out", (S, E), F32, kind="ExternalOutput").ap()
    build_program(nc, t, out)
    got = run_bass_kernel_spmd(nc, [arrays], core_ids=[0]).results[0]["out"]
    return got.reshape(1, S, E)
```
